# Optimizing a Trainium2 kernel written in Bass

```python
import numpy as np
import jax
import jax.numpy as jnp

def _softmax(x, axis=-1):
    return jax.nn.softmax(x, axis=axis)

def _gelu(x):
    return jax.nn.gelu(x, approximate=True)

def _silu(x):
    return jax.nn.silu(x)

def _sigmoid(x):
    return jax.nn.sigmoid(x)

def _layernorm(x, axis=-1, eps=1e-05):
    m = jnp.mean(x, axis=axis, keepdims=True)
    v = jnp.var(x, axis=axis, keepdims=True)
    return (x - m) / jnp.sqrt(v + eps)

def _scatter_add(tgt, idx, src, axis=0):
    return tgt.at[idx].add(src)

def _segment_sum(src, seg, n):
    return jax.ops.segment_sum(src, seg, n)
kernel_name = 'mk_gnn_preln_d1_gnn_r32_a978c8'

def setup_inputs(seed: int=0):
    np.random.seed(seed)
    _w = jnp.asarray

    def _rec_inputs():
        import jax
        import jax.numpy as jnp
        _gk = jax.random.key(seed)
        x = -0.000202 + 1 * jax.random.normal(jax.random.fold_in(_gk, 1), (3125, 64), jnp.float32)
        src = jax.random.randint(jax.random.fold_in(_gk, 2), (100000,), 0, 3125, jnp.int32)
        dst = jnp.minimum((3125 * jax.random.uniform(jax.random.fold_in(_gk, 3), (100000,)) ** 2.0).astype(jnp.int32), 99999)
        _o = jnp.argsort(dst, stable=True)
        src = src[_o]
        dst = dst[_o]
        edge_attr_64 = -5.16925e-05 + 1.00005 * jax.random.normal(jax.random.fold_in(_gk, 11), (100000, 64), jnp.float32)
        return (x, src, dst, edge_attr_64)
    x, src, dst, edge_attr_64 = _rec_inputs()

    def _L0_gnn_setup():
        import jax, jax.numpy as jnp
        import numpy as np
        N = 3125
        E = 50000
        C = 64
        H = 64
        L = 4
        EPS_MSG = 1e-07
        LN_EPS = 1e-05

        def _layernorm(x, g, b):
            mu = jnp.mean(x, axis=-1, keepdims=True)
            var = jnp.mean(jnp.square(x - mu), axis=-1, keepdims=True)
            return (x - mu) * jax.lax.rsqrt(var + LN_EPS) * g + b

        def _genconv(h, edge_attr, src, dst, w1, b1, g1, bb1, w2, b2, t):
            msg = jax.nn.relu(h[src] + edge_attr) + EPS_MSG
            m = msg * t
            seg_max = jax.lax.stop_gradient(jax.ops.segment_max(m, dst, num_segments=N))
            ex = jnp.exp(m - seg_max[dst])
            denom = jax.ops.segment_sum(ex, dst, num_segments=N)
            alpha = ex / (denom[dst] + 1e-16)
            agg = jax.ops.segment_sum(msg * alpha, dst, num_segments=N)
            out = h + agg
            z = jax.nn.relu(_layernorm(out @ w1 + b1, g1, bb1))
            return z @ w2 + b2
        key = jax.random.key(seed)
        ks = jax.random.split(key, 16)
        s = 0.05
        return {'x': jax.random.normal(ks[0], (N, C), jnp.float32), 'edge_index': jax.random.randint(ks[1], (2, E), 0, N, jnp.int32), 'edge_attr': jax.random.normal(ks[2], (E, C), jnp.float32), 'enc_node_w': jax.random.normal(ks[3], (C, H), jnp.float32) * s, 'enc_node_b': jnp.zeros((H,), jnp.float32), 'enc_edge_w': jax.random.normal(ks[4], (C, H), jnp.float32) * s, 'enc_edge_b': jnp.zeros((H,), jnp.float32), 'ln_g': jnp.ones((L, H), jnp.float32), 'ln_b': jnp.zeros((L, H), jnp.float32), 'mlp1_w': jax.random.normal(ks[5], (L, H, 2 * H), jnp.float32) * s, 'mlp1_b': jnp.zeros((L, 2 * H), jnp.float32), 'mlp_ln_g': jnp.ones((L, 2 * H), jnp.float32), 'mlp_ln_b': jnp.zeros((L, 2 * H), jnp.float32), 'mlp2_w': jax.random.normal(ks[6], (L, 2 * H, H), jnp.float32) * s, 'mlp2_b': jnp.zeros((L, H), jnp.float32), 't': jnp.ones((L,), jnp.float32)}
    _L0_gnn_all = _L0_gnn_setup()
    _L0_gnn_in = {k: v for k, v in _L0_gnn_all.items() if k in ('enc_node_w', 'enc_node_b', 'enc_edge_w', 'enc_edge_b', 'ln_g', 'ln_b', 'mlp1_w', 'mlp1_b', 'mlp_ln_g', 'mlp_ln_b', 'mlp2_w', 'mlp2_b', 't')}
    del _L0_gnn_all
    return {'x': x, 'src': src, 'dst': dst, 'edge_attr_64': edge_attr_64, 'L0_gnn_enc_node_w': _L0_gnn_in['enc_node_w'], 'L0_gnn_enc_node_b': _L0_gnn_in['enc_node_b'], 'L0_gnn_enc_edge_w': _L0_gnn_in['enc_edge_w'], 'L0_gnn_enc_edge_b': _L0_gnn_in['enc_edge_b'], 'L0_gnn_ln_g': _L0_gnn_in['ln_g'], 'L0_gnn_ln_b': _L0_gnn_in['ln_b'], 'L0_gnn_mlp1_w': _L0_gnn_in['mlp1_w'], 'L0_gnn_mlp1_b': _L0_gnn_in['mlp1_b'], 'L0_gnn_mlp_ln_g': _L0_gnn_in['mlp_ln_g'], 'L0_gnn_mlp_ln_b': _L0_gnn_in['mlp_ln_b'], 'L0_gnn_mlp2_w': _L0_gnn_in['mlp2_w'], 'L0_gnn_mlp2_b': _L0_gnn_in['mlp2_b'], 'L0_gnn_t': _L0_gnn_in['t']}

def reference(x, src, dst, edge_attr_64, L0_gnn_enc_node_w, L0_gnn_enc_node_b, L0_gnn_enc_edge_w, L0_gnn_enc_edge_b, L0_gnn_ln_g, L0_gnn_ln_b, L0_gnn_mlp1_w, L0_gnn_mlp1_b, L0_gnn_mlp_ln_g, L0_gnn_mlp_ln_b, L0_gnn_mlp2_w, L0_gnn_mlp2_b, L0_gnn_t):
    import jax
    import jax.numpy as jnp

    def _L0_gnn_ref(x, edge_index, edge_attr, enc_node_w, enc_node_b, enc_edge_w, enc_edge_b, ln_g, ln_b, mlp1_w, mlp1_b, mlp_ln_g, mlp_ln_b, mlp2_w, mlp2_b, t):
        import jax, jax.numpy as jnp
        import numpy as np
        N = 3125
        E = 50000
        C = 64
        H = 64
        L = 4
        EPS_MSG = 1e-07
        LN_EPS = 1e-05

        def _layernorm(x, g, b):
            mu = jnp.mean(x, axis=-1, keepdims=True)
            var = jnp.mean(jnp.square(x - mu), axis=-1, keepdims=True)
            return (x - mu) * jax.lax.rsqrt(var + LN_EPS) * g + b

        def _genconv(h, edge_attr, src, dst, w1, b1, g1, bb1, w2, b2, t):
            msg = jax.nn.relu(h[src] + edge_attr) + EPS_MSG
            m = msg * t
            seg_max = jax.lax.stop_gradient(jax.ops.segment_max(m, dst, num_segments=N))
            ex = jnp.exp(m - seg_max[dst])
            denom = jax.ops.segment_sum(ex, dst, num_segments=N)
            alpha = ex / (denom[dst] + 1e-16)
            agg = jax.ops.segment_sum(msg * alpha, dst, num_segments=N)
            out = h + agg
            z = jax.nn.relu(_layernorm(out @ w1 + b1, g1, bb1))
            return z @ w2 + b2
        src, dst = (edge_index[0], edge_index[1])
        h = x @ enc_node_w + enc_node_b
        e = edge_attr @ enc_edge_w + enc_edge_b
        h = _genconv(h, e, src, dst, mlp1_w[0], mlp1_b[0], mlp_ln_g[0], mlp_ln_b[0], mlp2_w[0], mlp2_b[0], t[0])
        for i in range(1, L):
            z = jax.nn.relu(_layernorm(h, ln_g[i], ln_b[i]))
            h = h + _genconv(z, e, src, dst, mlp1_w[i], mlp1_b[i], mlp_ln_g[i], mlp_ln_b[i], mlp2_w[i], mlp2_b[i], t[i])
        return jax.nn.relu(_layernorm(h, ln_g[0], ln_b[0]))
    edge_index = jnp.stack([src, dst])
    h = jnp.maximum(_layernorm(x, axis=-1), 0.0)
    x = x + _L0_gnn_ref(h, edge_index, edge_attr_64, L0_gnn_enc_node_w, L0_gnn_enc_node_b, L0_gnn_enc_edge_w, L0_gnn_enc_edge_b, L0_gnn_ln_g, L0_gnn_ln_b, L0_gnn_mlp1_w, L0_gnn_mlp1_b, L0_gnn_mlp_ln_g, L0_gnn_mlp_ln_b, L0_gnn_mlp2_w, L0_gnn_mlp2_b, L0_gnn_t)
    return x

_drawn_inputs = setup_inputs


def setup_inputs(seed=0):
    import zlib

    import numpy as np

    out = dict(_drawn_inputs(seed))
    spreads = {'L0_gnn_enc_node_b': (0.0, 0.1),
     'L0_gnn_enc_edge_b': (0.0, 0.1),
     'L0_gnn_ln_g': (1.0, 0.2),
     'L0_gnn_ln_b': (0.0, 0.1),
     'L0_gnn_mlp1_b': (0.0, 0.1),
     'L0_gnn_mlp_ln_g': (1.0, 0.2),
     'L0_gnn_mlp_ln_b': (0.0, 0.1),
     'L0_gnn_mlp2_b': (0.0, 0.1),
     'L0_gnn_t': (1.0, 0.2)}
    factors = {}
    for name, (base, spread) in spreads.items():
        noise = np.random.default_rng([zlib.crc32(name.encode()), seed]).standard_normal(out[name].shape)
        drawn = base * np.exp(spread * noise) if base else spread * noise
        out[name] = jnp.asarray(drawn.astype(out[name].dtype))
    for name, factor in factors.items():
        out[name] = (out[name] * factor).astype(out[name].dtype)
    return out
```

```python
import concourse.bass as bass
from concourse import mybir
from contextlib import ExitStack

F32 = mybir.dt.float32
BF16 = mybir.dt.bfloat16
I32 = mybir.dt.int32
U32 = mybir.dt.uint32
ALU = mybir.AluOpType
ACT = mybir.ActivationFunctionType
AX = mybir.AxisListType

N, H, E, L = 3125, 64, 100000, 4
H2 = 2 * H
MSG_EPS, DEN_EPS, LN_EPS = 1e-07, 1e-16, 1e-05
ROUND = 12582912.0
FAR = -1.0e30

P = 128
SUB = 4
CH = P * SUB
NCH = 98
HALF = NCH * CH
HALF_AT = E - HALF
assert HALF_AT <= HALF and NCH % 2 == 0
CUT_COL = (HALF_AT - 1) - (NCH - 1) * CH
assert 0 <= CUT_COL < CH
SW_SHIFT = HALF - HALF_AT

NP, NK = 125, 25
assert NP * NK == N
GW = 4
GROUPS = [(k, min(GW, NK - k)) for k in range(0, NK, GW)]
NG = len(GROUPS)
ECOLS = E // NP
HB = 16
NHB = ECOLS // HB
assert NHB % 2 == 0 and NHB * HB == ECOLS
PRE = 2


def program(nc, x, src, dst, attr, enc_w, enc_b, edge_w, edge_b, ln_g, ln_b, w1, b1, g1, bb1, w2, b2, t, out):
    ctx = ExitStack()
    with ctx:
        ctx.enter_context(nc.allow_non_contiguous_dma(reason="columns of parameters"))

        def sb(name, shape, dt=F32):
            return ctx.enter_context(nc.sbuf_tensor(name, shape, dt))

        def pb(name, shape, dt=F32):
            return ctx.enter_context(nc.psum_tensor(name, shape, dt))

        def sem(name):
            return ctx.enter_context(nc.semaphore(name))

        z_rows = nc.dram_tensor("z_rows", (N, H), F32, kind="Internal").ap()
        sw_rows = nc.dram_tensor("sw_rows", (2 * HALF, 2 * H), F32, kind="Internal").ap()
        max_cols = nc.dram_tensor("max_cols", (H, HALF), F32, kind="Internal").ap()
        fall_rows = nc.dram_tensor("fall_rows", (2, HALF), BF16, kind="Internal").ap()

        ident = sb("ident", [P, P])
        half_sel = sb("half_sel", [2, P], BF16)
        below = sb("below", [NP, NP])
        edge_w2 = sb("edge_w2", [P, P])
        edge_b2 = sb("edge_b2", [P, 1])
        t_all = sb("t_all", [P, L])
        enc_wb = sb("enc_wb", [H + 1, H])
        w1b = sb("w1b", [H + 1, L, H2])
        w2_all = sb("w2_all", [H2, L, H])
        g1_all = sb("g1_all", [H2, L])
        bb1_all = sb("bb1_all", [H2, L])
        b2_all = sb("b2_all", [NP, L, H])
        lng_all = sb("lng_all", [NP, L, H])
        lnb_all = sb("lnb_all", [NP, L, H])
        t_now = sb("t_now", [P, 1])
        w1_now = sb("w1_now", [H + 1, H2])
        w2_now = sb("w2_now", [H2, H])
        g1_now = sb("g1_now", [H2, 1])
        bb1_now = sb("bb1_now", [H2, 1])
        b2_now = sb("b2_now", [NP, H])
        lng_now = sb("lng_now", [NP, H])
        lnb_now = sb("lnb_now", [NP, H])

        src_idx = sb("src_idx", [P, NCH, 2, SUB], I32)
        idx_now = [sb(f"idx_now{s}", [P, 2 * SUB], I32) for s in range(2)]
        row_idx = sb("row_idx", [NP, NK], I32)
        has_edges = sb("has_edges", [NP, NK])
        seam_end = sb("seam_end", [1, 1], I32)
        seam_fall = sb("seam_fall", [H, 1])

        def two(name, shape, dt=F32):
            return [sb(f"{name}{s}", shape, dt) for s in range(2)]

        attr_in = two("attr_in", [P, SUB, 2, H])
        fall_in = two("fall_in", [2, CH], BF16)
        zsrc = two("zsrc", [P, SUB, 2, H])
        attr_t = two("attr_t", [P, CH])
        r = two("r", [P, CH])
        du = two("du", [P, 2, CH])
        ex = two("ex", [P, 2, CH])
        rex = sb("rex", [P, CH])
        M = two("M", [P, CH + 1])
        S = two("S", [P, CH])
        W = two("W", [P, CH])
        sw_out = two("sw_out", [P, 2, SUB, 2, H])

        seam_m = sb("seam_m", [H, 2])
        seam_x = sb("seam_x", [H, 1])
        seam_e = sb("seam_e", [H, 2])
        seam_sw1 = sb("seam_sw1", [H, 2])
        seam_sw = sb("seam_sw", [H, 2])

        node_sw = sb("node_sw", [NP, NK, 2, H])
        z = sb("z", [NP, NK, H])
        hres = sb("hres", [NP, NK, H])
        x_in = sb("x_in", [NP, NK, H])
        agg = two("agg", [NP, GW, H])
        rden = sb("rden", [NP, GW, H])
        node_t = two("node_t", [H + 1, GW * NP])
        stats = sb("stats", [NP, GW, 6])
        mv1 = two("mv1", [NP, GW, 2])
        sd1 = two("sd1", [NP, GW])
        rs1 = sb("rs1", [NP, GW])
        y_hat = two("y_hat", [NP, GW, H2])
        hid_t = two("hid_t", [H2, GW * NP])
        stats2 = sb("stats2", [NP, GW, 6])
        mv2 = two("mv2", [NP, GW, 2])
        sd2 = two("sd2", [NP, GW])
        rs2 = sb("rs2", [NP, GW])
        eps_col = sb("eps_col", [P, 1])
        zero_col = sb("zero_col", [P, 1])

        dst_win = sb("dst_win", [NCH, 2, CH + 1], I32)
        fall_sb = sb("fall_sb", [NCH, 2, CH], BF16)
        dst_cols = sb("dst_cols", [NP, ECOLS], I32)
        dst_f = sb("dst_f", [NP, ECOLS])
        hi_f = sb("hi_f", [NP, ECOLS])
        hi_b = sb("hi_b", [NP, ECOLS], BF16)
        lo_b = sb("lo_b", [NP, ECOLS], BF16)
        count_i = sb("count_i", [NP, NP], I32)
        count_b = sb("count_b", [NP, NP], BF16)
        hot_hi = two("hot_hi", [NP, HB, NP], BF16)
        hot_lo = two("hot_lo", [NP, HB, NK], BF16)
        hist = sb("hist", [NP, NK])
        hist_sum = sb("hist_sum", [NP, 1])
        cum = sb("cum", [NP, NK])
        scr = sb("scr", [NP, NK])
        scr2 = sb("scr2", [NP, NK])
        seam_col = sb("seam_col", [NP, 1])
        seam_row = sb("seam_row", [1, 4])
        seam_dst = sb("seam_dst", [H, 2], I32)
        zeros_b = sb("zeros_b", [NP, NP], BF16)
        xn = sb("xn", [NP, NK, H])
        stats_all = sb("stats_all", [NP, NK, 6])
        mv_all = sb("mv_all", [NP, NK, 2])
        dst_d = sb("dst_d", [NCH, 2, CH])

        pA = [pb(f"pA{s}", [P, CH]) for s in range(2)]
        pX = [pb(f"pX{s}", [P, CH]) for s in range(2)]
        pR = [pb(f"pR{s}", [P, CH]) for s in range(2)]
        pT = [pb(f"pT{s}", [P, CH]) for s in range(2)]

        par_in = sem("par_in")
        idx_in = sem("idx_in")
        dst_in = sem("dst_in")
        x_loaded = sem("x_loaded")
        consts = sem("consts")
        dve_consts = sem("dve_consts")
        fall_ready, fall_stored = sem("fall_ready"), sem("fall_stored")
        hot_ready, hot_used, hist_done, cum_step, cum_mm = (sem(n) for n in ("hot_ready", "hot_used", "hist_done", "cum_step", "cum_mm"))
        seam_known = sem("seam_known")
        enc_in, enc_tp, enc_sb, enc_mm, enc_out = (sem(n) for n in ("enc_in", "enc_tp", "enc_sb", "enc_mm", "enc_out"))
        z_ready, z_stored = sem("z_ready"), sem("z_stored")
        layer_par = sem("layer_par")
        idx_staged = sem("idx_staged")
        loads = [sem(f"loads{s}") for s in range(2)]
        gathered = [sem(f"gathered{s}") for s in range(2)]
        m_stored = [sem(f"m_stored{s}") for s in range(2)]
        sw_stored = [sem(f"sw_stored{s}") for s in range(2)]
        attr_tp = sem("attr_tp")
        attr_sb = sem("attr_sb")
        x_mm = sem("x_mm")
        r_done = sem("r_done")
        u_done = sem("u_done")
        m_done = sem("m_done")
        d_done = sem("d_done")
        du_done = sem("du_done")
        ex_done = sem("ex_done")
        rex_done = sem("rex_done")
        sw_done = sem("sw_done")
        back_tp = sem("back_tp")
        back_sb = sem("back_sb")
        seam_in, seam_max, seam_exp, seam_done, seam_stored = (sem(n) for n in ("seam_in", "seam_max", "seam_exp", "seam_done", "seam_stored"))
        node_in = [sem(f"node_in{j}") for j in range(NG)]
        agg_done = sem("agg_done")
        node_tp = sem("node_tp")
        node_t_sb = sem("node_t_sb")
        y_mm = sem("y_mm")
        mv1_done = sem("mv1_done")
        sd1_done = sem("sd1_done")
        y_hat_done = sem("y_hat_done")
        hat_tp = sem("hat_tp")
        hid_done = sem("hid_done")
        o_mm = sem("o_mm")
        mv2_done = sem("mv2_done")
        sd2_done = sem("sd2_done")
        out_ready, out_stored = sem("out_ready"), sem("out_stored")

        sp_passed, pool_passed, pe_passed = sem("sp_passed"), sem("pool_passed"), sem("pe_passed")

        N_PAR = 2 + 9 + 4 + 2

        def done(turn):
            return turn + (1 + PRE)

        def edge_rows(ap, h, first):
            return ap[bass.ds(first, CH), :].rearrange("(p t) c -> p t c", t=SUB)

        block = ctx.enter_context(nc.Block())

        @block.sync
        def _(sp):
            sp.dma_start(x_in[:, :, :], x.rearrange("(p k) c -> p k c", k=NK)).then_inc(x_loaded, 16)
            sp.dma_start(dst_cols[:, :], dst.rearrange("(p c) -> p c", c=ECOLS)).then_inc(dst_in, 16)
            for h in range(2):
                first = h * HALF_AT
                sp.dma_start(dst_win[:, h, 1:], dst[first:first + HALF].rearrange("(q j) -> q j", j=CH)).then_inc(dst_in, 16)
            for h in range(2):
                first = h * HALF_AT
                tail = dst[first:first + HALF - CH].rearrange("(q j) -> q j", j=CH)
                sp.dma_start(dst_win[1:NCH, h, 0:1], tail[:, CH - 1:CH]).then_inc(dst_in, 16)
            sp.dma_start(seam_dst[:, :], dst[HALF_AT - 1:HALF_AT + 1][None, :].to_broadcast([H, 2])).then_inc(dst_in, 16)

            sp.wait_ge(fall_ready, 1)
            for h in range(2):
                sp.dma_start(fall_rows[h, :].rearrange("(q j) -> q j", j=CH), fall_sb[:, h, :]).then_inc(fall_stored, 16)
            sp.wait_ge(fall_stored, 32)

            def load(first_edge, s):
                for h in range(2):
                    sp.dma_start(attr_in[s][:, :, h, :], edge_rows(attr, h, first_edge + h * HALF_AT)).then_inc(loads[s], 16)
                sp.dma_start(fall_in[s][:, :], fall_rows[:, bass.ds(first_edge, CH)]).then_inc(loads[s], 16)

            def store_m(first_edge, s, g):
                sp.wait_ge(m_done, done(g))
                sp.sem_inc(sp_passed, 1)
                sp.dma_start(max_cols[:, bass.ds(first_edge, CH)], M[s][H:P, 1:CH + 1]).then_inc(m_stored[s], 16)

            def store_sw(first_edge, s, g):
                sp.wait_ge(back_sb, 2 * g + 2 * (1 + PRE))
                for h in range(2):
                    sp.dma_start(edge_rows(sw_rows, h, first_edge + h * HALF).rearrange("p t c -> p (t c)"),
                                 sw_out[s][:, h, :, :, :].rearrange("p t s c -> p (t s c)")).then_inc(sw_stored[s], 16)

            for s in range(2):
                sp.sem_inc(m_stored[s], 16)
                sp.sem_inc(sw_stored[s], 32)
                load(s * CH, s)

            sp.wait_ge(z_ready, 1)
            sp.dma_start(z_rows.rearrange("(p k) c -> p k c", k=NK), z[:, :, :]).then_inc(z_stored, 16)
            sp.wait_ge(seam_known, 1)
            seam_at = sp.value_load(seam_end[0:1, 0:1], min_val=0, max_val=HALF - 1)

            with sp.Fori(0, L) as l:
                def step(first, g, s, load_at=None, sw=True):
                    sp.wait_ge(attr_tp, done(g))
                    load(first + 2 * CH if load_at is None else load_at, s)
                    store_m(first, s, g)
                    if sw:
                        store_sw(first - 2 * CH, s, g - 2)

                g0 = sp.snap(l * NCH)
                for c in range(2):
                    step(c * CH, g0 + c, c, sw=False)
                with sp.Fori(1, NCH // 2 - 1) as i:
                    first, g = sp.snap(i * (2 * CH)), sp.snap(g0 + i * 2)
                    for s in range(2):
                        step(first + s * CH, g + s, s)
                for c in range(NCH - 2, NCH):
                    step(c * CH, g0 + c, c % 2, load_at=(c % 2) * CH)
                for c in range(NCH - 2, NCH):
                    store_sw(c * CH, c % 2, g0 + c)
                q = sp.snap(l * (NCH // 2))
                for s in range(2):
                    sp.wait_ge(sw_stored[s], q * 32 + 32 * (NCH // 2 + 1))
                    sp.wait_ge(m_stored[s], q * 16 + 16 * (NCH // 2 + 1))
                sp.sem_inc(sp_passed, 1)
                sp.dma_start(seam_m[:, 1:2], max_cols[:, bass.ds(seam_at, 1)]).then_inc(seam_in, 16)
                seam_row_ap = sw_rows[bass.ds(seam_at + HALF, 1), :].rearrange("o (s c) -> c (o s)", s=2)
                sp.dma_start(seam_sw1[:, :], seam_row_ap).then_inc(seam_in, 16)
                sp.wait_ge(seam_done, l + 1)
                sp.dma_start(sw_rows[bass.ds(seam_at + HALF, 1), :].rearrange("o (s c) -> c (o s)", s=2),
                             seam_sw[:, :]).then_inc(seam_stored, 16)
                sp.wait_ge(z_ready, l + 2)
                sp.dma_start(z_rows.rearrange("(p k) c -> p k c", k=NK), z[:, :, :]).then_inc(z_stored, 16)
            sp.wait_ge(z_stored, 16 * (L + 1))
            sp.wait_ge(out_ready, 1)
            sp.dma_start(out.rearrange("(p k) c -> p k c", k=NK), x_in[:, :, :]).then_inc(out_stored, 16)
            for s in range(2):
                sp.wait_ge(loads[s], 48 * (L * NCH // 2 + 1))
            sp.wait_ge(out_stored, 16)

        @block.gpsimd
        def _(pool):
            pool.memset(ident[:, :], 0.0).then_inc(consts, 1)
            pool.memset(below[:, :], 0.0).then_inc(consts, 1)
            pool.memset(half_sel[:, :], 0.0).then_inc(consts, 1)
            pool.wait_ge(consts, 3)
            pool.affine_select(out=ident[:, :], in_=ident[:, :], compare_op=ALU.not_equal, fill=1.0, base=0,
                               pattern=[[-1, P]], channel_multiplier=1).then_inc(consts, 1)
            pool.affine_select(out=below[:, :], in_=below[:, :], compare_op=ALU.is_ge, fill=1.0, base=0,
                               pattern=[[-1, NP]], channel_multiplier=1).then_inc(consts, 1)
            pool.affine_select(out=half_sel[:, :].rearrange("p (m c) -> p m c", c=H),
                               in_=half_sel[:, :].rearrange("p (m c) -> p m c", c=H), compare_op=ALU.not_equal,
                               fill=1.0, base=0, pattern=[[-1, 2], [0, H]], channel_multiplier=1).then_inc(consts, 1)
            pool.iota(count_i[:, :], pattern=[[1, NP]], base=0, channel_multiplier=0).then_inc(consts, 1)
            pool.wait_ge(idx_in, 32)
            with pool.Fori(0, L) as l:
                pool.wait_ge(z_stored, l * 16 + 16)
                pool.sem_inc(pool_passed, 1)
                with pool.Fori(0, NCH // 2) as i:
                    g = pool.snap(l * NCH + i * 2)
                    for s in range(2):
                        pool.wait_ge(x_mm, done(g + (s - 2)))
                        pool.tensor_copy(idx_now[s][:, :], src_idx[:, bass.ds(i * 2 + s, 1), :, :].rearrange("p o h t -> p (o h t)")).then_inc(idx_staged, 1)
                        pool.wait_ge(idx_staged, g + (s + 1))
                        pool.sem_inc(pool_passed, 1)
                        for h in range(2):
                            for t4 in range(SUB):
                                at = h * SUB + t4
                                pool.indirect_dma_start(
                                    zsrc[s][:, t4, h, :], None, z_rows,
                                    bass.IndirectOffsetOnAxis(idx_now[s][:, at:at + 1].bitcast(U32), 0)).then_inc(gathered[s], 16)
                pool.wait_ge(seam_stored, l * 16 + 16)
                pool.sem_inc(pool_passed, 1)
                for j, (k0, w) in enumerate(GROUPS):
                    for k in range(k0, k0 + w):
                        pool.indirect_dma_start(
                            node_sw[:, k, :, :].rearrange("p s c -> p (s c)"), None, sw_rows,
                            bass.IndirectOffsetOnAxis(row_idx[:, k:k + 1].bitcast(U32), 0)).then_inc(node_in[j], 16)

        @block.scalar
        def _(act):
            for h in range(2):
                rows = slice(h * H, h * H + H)
                first = h * HALF_AT
                act.dma_start(src_idx[:, :, h, :], src[first:first + HALF].rearrange("(c p t) -> p c t", p=P, t=SUB)).then_inc(idx_in, 16)
                act.dma_start(edge_b2[rows, :], edge_b[:, None]).then_inc(par_in, 16)
            act.dma_start(t_all[:, :], t[None, :].to_broadcast([P, L])).then_inc(par_in, 16)
            act.dma_start(enc_wb[0:H, :], enc_w).then_inc(par_in, 16)
            act.dma_start(enc_wb[H:H + 1, :], enc_b[None, :]).then_inc(par_in, 16)
            act.dma_start(w1b[0:H, :, :], w1.rearrange("l c n -> c l n")).then_inc(par_in, 16)
            act.dma_start(w1b[H:H + 1, :, :], b1[None, :, :]).then_inc(par_in, 16)
            act.dma_start(w2_all[:, :, :], w2.rearrange("l c n -> c l n")).then_inc(par_in, 16)
            act.dma_start(g1_all[:, :], g1.rearrange("l c -> c l")).then_inc(par_in, 16)
            act.dma_start(bb1_all[:, :], bb1.rearrange("l c -> c l")).then_inc(par_in, 16)
            act.dma_start(b2_all[:, :, :], b2[None, :, :].to_broadcast([NP, L, H])).then_inc(par_in, 16)
            for all_, dram in ((lng_all, ln_g), (lnb_all, ln_b)):
                act.dma_start(all_[:, 0:L - 1, :], dram[None, 1:L, :].to_broadcast([NP, L - 1, H])).then_inc(par_in, 16)
                act.dma_start(all_[:, L - 1:L, :], dram[None, 0:1, :].to_broadcast([NP, 1, H])).then_inc(par_in, 16)
            act.wait_ge(dve_consts, 1)
            for h in range(2):
                rows = slice(h * H, h * H + H)
                act.dma_start(edge_w2[rows, rows], edge_w).then_inc(par_in, 16)

            act.wait_ge(enc_in, 1)
            act.activation(scr2[:, :], scr[:, :], ACT.Sqrt, bias=eps_col[0:NP, :]).then_inc(enc_in, 1)
            for j, (k0, w) in enumerate(GROUPS):
                act.wait_ge(enc_tp, j + 1)
                if j >= 2:
                    act.wait_ge(enc_mm, j - 1)
                act.activation(node_t[j % 2][0:H, 0:w * NP], pA[j % 2][0:H, 0:w * NP], ACT.Copy).then_inc(enc_sb, 1)

            act.sem_inc(attr_sb, PRE)
            act.sem_inc(r_done, PRE)
            act.sem_inc(u_done, PRE)
            act.sem_inc(ex_done, PRE)
            act.sem_inc(back_sb, 2 * PRE)
            act.sem_inc(node_t_sb, PRE)
            act.sem_inc(sd1_done, PRE)
            act.sem_inc(hid_done, PRE)
            act.sem_inc(sd2_done, PRE)

            with act.Fori(0, L) as l:
                act.wait_ge(layer_par, l + 1)

                def messages(s, g):
                    act.wait_ge(attr_tp, done(g))
                    act.activation(attr_t[s][:, :], pA[s][:, :], ACT.Copy).then_inc(attr_sb, 1)
                    act.wait_ge(x_mm, done(g))
                    act.wait_ge(rex_done, done(g - 2))
                    act.activation(r[s][:, :], pX[s][:, :], ACT.Relu, bias=edge_b2[:, :]).then_inc(r_done, 1)
                    act.wait_ge(r_done, done(g))
                    act.activation(du[s][:, 1, :], r[s][:, :], ACT.Copy, scale=t_now[:, 0:1]).then_inc(u_done, 1)

                def exps(s, g):
                    act.wait_ge(du_done, done(g))
                    act.activation(ex[s][:, :, :], du[s][:, :, :], ACT.Exp).then_inc(ex_done, 1)

                def copy_out(s, g, q):
                    act.wait_ge(sw_stored[s], q * 32 + 32)
                    for b in range(2):
                        act.wait_ge(back_tp, 2 * g + (2 * PRE + b + 1))
                        act.activation(sw_out[s][:, :, 2 * b:2 * b + 2, :, :].rearrange("p h t s c -> p (t s) h c"),
                                       pT[b][:, :].rearrange("p (a h c) -> p a h c", a=4, h=2), ACT.Copy).then_inc(back_sb, 1)

                def step(c, g, q, a=True, e=True, o=True):
                    if a:
                        messages((c + 1) % 2, g + (c + 1))
                    if o:
                        copy_out(c % 2, g + (c - 2), q + (c - 2) // 2)
                    if e:
                        exps(c % 2, g + c)

                g0, q0 = act.snap(l * NCH), act.snap(l * (NCH // 2))
                step(-1, g0, q0, e=False, o=False)
                for c in range(2):
                    step(c, g0, q0, o=False)
                with act.Fori(1, NCH // 2 - 1) as i:
                    g, q = act.snap(g0 + i * 2), act.snap(q0 + i)
                    for c in range(2):
                        step(c, g, q)
                step(NCH - 2, g0, q0)
                step(NCH - 1, g0, q0, a=False)
                step(NCH, g0, q0, a=False, e=False)
                step(NCH + 1, g0, q0, a=False, e=False)

                act.wait_ge(seam_max, l + 1)
                act.activation(seam_e[:, :], seam_m[:, :], ACT.Exp).then_inc(seam_exp, 1)

                G0 = act.snap(l * NG)

                def to_sb(j):
                    act.wait_ge(node_tp, done(G0 + j))
                    act.wait_ge(y_mm, done(G0 + (j - 2)))
                    w = GROUPS[j][1]
                    act.activation(node_t[j % 2][0:H, 0:w * NP], pA[j % 2][0:H, 0:w * NP], ACT.Copy).then_inc(node_t_sb, 1)

                def deviation(j, mv, sd, ready, signal):
                    act.wait_ge(ready, done(G0 + j))
                    w = GROUPS[j][1]
                    act.activation(sd[j % 2][:, 0:w], mv[j % 2][:, 0:w, 1], ACT.Sqrt, bias=eps_col[0:NP, :]).then_inc(signal, 1)

                def hidden(j):
                    act.wait_ge(hat_tp, done(G0 + j))
                    act.wait_ge(o_mm, done(G0 + (j - 2)))
                    w = GROUPS[j][1]
                    act.activation(hid_t[j % 2][:, 0:w * NP], pT[j % 2][:, 0:w * NP], ACT.Relu,
                                   bias=bb1_now[:, :], scale=g1_now[:, :]).then_inc(hid_done, 1)

                to_sb(0)
                for j in range(NG + 1):
                    if j + 1 < NG:
                        to_sb(j + 1)
                    if j < NG:
                        deviation(j, mv1, sd1, mv1_done, sd1_done)
                    if j >= 1:
                        deviation(j - 1, mv2, sd2, mv2_done, sd2_done)
                    if j < NG:
                        hidden(j)

        @block.tensor
        def _(pe):
            pe.wait_ge(consts, 7)
            pe.wait_ge(dve_consts, 5)
            pe.wait_ge(par_in, 16 * N_PAR)
            for j, (k0, w) in enumerate(GROUPS):
                pe.wait_ge(enc_in, 3)
                if j >= 2:
                    pe.wait_ge(enc_sb, j - 1)
                for k in range(w):
                    last = pe.transpose(pA[j % 2][0:H, k * NP:(k + 1) * NP], xn[:, k0 + k, :], ident[0:NP, 0:NP])
                last.then_inc(enc_tp, 1)
                pe.wait_ge(enc_sb, j + 1)
                if j >= 2:
                    pe.wait_ge(enc_out, j - 1)
                for k in range(w):
                    last = pe.matmul(pX[j % 2][0:NP, k * H:(k + 1) * H], node_t[j % 2][:, k * NP:(k + 1) * NP],
                                     enc_wb[:, :], start=True, stop=True)
                last.then_inc(enc_mm, 1)

            pe.matmul(pT[0][0:NP, 0:NK], zeros_b[:, :], zeros_b[:, 0:NK], start=True, stop=False, skip_group_check=True)
            with pe.Fori(0, NHB // 2) as i:
                b = pe.snap(i * 2)
                for s in range(2):
                    pe.wait_ge(hot_ready, b + (s + 1))
                    for c in range(HB):
                        last = pe.matmul(pT[0][0:NP, 0:NK], hot_hi[s][:, c, :], hot_lo[s][:, c, :],
                                         start=False, stop=False, skip_group_check=True)
                    last.then_inc(hot_used, 1)
            pe.matmul(pT[0][0:NP, 0:NK], zeros_b[:, :], zeros_b[:, 0:NK], start=False, stop=True,
                      skip_group_check=True).then_inc(hist_done, 1)
            pe.wait_ge(cum_step, 1)
            pe.matmul(pT[1][0:NP, 0:1], below[:, :], hist_sum[:, :], start=True, stop=True).then_inc(cum_mm, 1)
            pe.wait_ge(cum_step, 2)
            pe.transpose(pT[1][0:1, 0:NP], seam_col[:, :], ident[0:NP, 0:NP]).then_inc(cum_mm, 1)

            pe.sem_inc(attr_tp, PRE)
            pe.sem_inc(x_mm, PRE)
            pe.sem_inc(back_tp, 2 * PRE)
            pe.sem_inc(node_tp, PRE)
            pe.sem_inc(y_mm, PRE)
            pe.sem_inc(hat_tp, PRE)
            pe.sem_inc(o_mm, PRE)

            with pe.Fori(0, L) as l:
                pe.wait_ge(z_ready, l + 1)

                def front(s, g, q):
                    pe.wait_ge(loads[s], q * 48 + 48)
                    pe.wait_ge(d_done, done(g - 2))
                    pe.matmul(pR[s][:, :], half_sel[:, :], fall_in[s][:, :], start=True, stop=True)
                    for t4 in range(SUB):
                        last = pe.transpose(pA[s][:, t4:CH:SUB], attr_in[s][:, t4, :, :].rearrange("p h c -> p (h c)"), ident[:, :])
                    last.then_inc(attr_tp, 1)
                    pe.wait_ge(attr_sb, done(g))
                    pe.matmul(pX[s][:, :], edge_w2[:, :], attr_t[s][:, :], start=True, stop=False, skip_group_check=True)
                    pe.wait_ge(gathered[s], q * 128 + 128)
                    for t4 in range(SUB):
                        last = pe.matmul(pX[s][:, t4:CH:SUB], zsrc[s][:, t4, :, :].rearrange("p h c -> p (h c)"), ident[:, :],
                                         start=False, stop=(t4 == SUB - 1), skip_group_check=True)
                    last.then_inc(x_mm, 1)

                def back(s, g):
                    pe.wait_ge(sw_done, done(g))
                    for b in range(2):
                        pe.wait_ge(back_sb, 2 * g + (2 * PRE + b - 1))
                        for t4 in range(2 * b, 2 * b + 2):
                            for n, scanned in enumerate((S, W)):
                                at = ((t4 % 2) * 2 + n) * P
                                last = pe.transpose(pT[b][:, at:at + P], scanned[s][:, t4:CH:SUB], ident[:, :])
                        last.then_inc(back_tp, 1)

                def step(c, g, q, a=True, o=True):
                    if a:
                        front((c + 1) % 2, g + (c + 1), q + (c + 1) // 2)
                    if o:
                        back(c % 2, g + (c - 2))

                g0, q0 = pe.snap(l * NCH), pe.snap(l * (NCH // 2))
                for c in range(-1, 2):
                    step(c, g0, q0, o=False)
                with pe.Fori(1, NCH // 2 - 1) as i:
                    g, q = pe.snap(g0 + i * 2), pe.snap(q0 + i)
                    for c in range(2):
                        step(c, g, q)
                step(NCH - 2, g0, q0)
                for c in range(NCH - 1, NCH + 2):
                    step(c, g0, q0, a=False)

                G0 = pe.snap(l * NG)

                def first_half(j):
                    k0, w = GROUPS[j]
                    pe.wait_ge(agg_done, done(G0 + j))
                    pe.wait_ge(node_t_sb, done(G0 + (j - 2)))
                    pe.sem_inc(pe_passed, 1)
                    for k in range(w):
                        last = pe.transpose(pA[j % 2][0:H, k * NP:(k + 1) * NP], agg[j % 2][:, k, :], ident[0:NP, 0:NP])
                    last.then_inc(node_tp, 1)
                    pe.wait_ge(node_t_sb, done(G0 + j))
                    pe.wait_ge(y_hat_done, done(G0 + (j - 2)))
                    for k in range(w):
                        last = pe.matmul(pX[j % 2][0:NP, k * H2:(k + 1) * H2], node_t[j % 2][:, k * NP:(k + 1) * NP],
                                         w1_now[:, :], start=True, stop=True)
                    last.then_inc(y_mm, 1)

                def second_half(j):
                    k0, w = GROUPS[j]
                    pe.wait_ge(y_hat_done, done(G0 + j))
                    if j < 2:
                        pe.wait_ge(back_sb, 2 * g0 + 2 * (NCH + PRE))
                    else:
                        pe.wait_ge(hid_done, done(G0 + (j - 2)))
                    for k in range(w):
                        last = pe.transpose(pT[j % 2][:, k * NP:(k + 1) * NP], y_hat[j % 2][:, k, :], ident[0:NP, 0:NP])
                    last.then_inc(hat_tp, 1)
                    pe.wait_ge(hid_done, done(G0 + j))
                    pe.wait_ge(mv2_done, done(G0 + (j - 2)))
                    for k in range(w):
                        last = pe.matmul(pR[j % 2][0:NP, k * H:(k + 1) * H], hid_t[j % 2][:, k * NP:(k + 1) * NP],
                                         w2_now[:, :], start=True, stop=True)
                    last.then_inc(o_mm, 1)

                first_half(0)
                for j in range(NG):
                    if j + 1 < NG:
                        first_half(j + 1)
                    second_half(j)

        @block.vector
        def _(dve):
            v = nc.vector
            v.memset(edge_w2[:, :], 0.0).then_inc(dve_consts, 1)
            v.memset(eps_col[:, :], LN_EPS).then_inc(dve_consts, 1)
            dve.wait_ge(consts, 7)
            v.tensor_copy(count_b[:, :], count_i[:, :])
            v.memset(zeros_b[:, :], 0.0).then_inc(dve_consts, 1)
            for s in range(2):
                v.memset(node_t[s][H:H + 1, :], 1.0).then_inc(dve_consts, 1)
            v.memset(dst_win[0:1, :, 0:1], -1)
            v.memset(hres[:, :, :], 0.0)
            for s in range(2):
                v.memset(M[s][:, :], 0.0)
                v.memset(S[s][:, :], 0.0)
                v.memset(W[s][:, :], 0.0)

            dve.wait_ge(x_loaded, 16)
            for k in range(NK):
                v.bn_stats(stats_all[:, k, :], x_in[:, k, :])
            dve.drain()
            for k in range(NK):
                v.bn_aggr(mv_all[:, k, :], stats_all[:, k, :])
            dve.drain()
            v.tensor_copy(scr[:, :], mv_all[:, :, 1]).then_inc(enc_in, 1)
            dve.wait_ge(enc_in, 2)
            v.reciprocal(scr2[:, :], scr2[:, :])
            dve.drain()
            for k in range(NK):
                v.tensor_scalar(xn[:, k, :], x_in[:, k, :], mv_all[:, k, 0:1], scr2[:, k:k + 1], ALU.subtract, ALU.mult)
            dve.drain()
            v.tensor_scalar_max(xn[:, :, :], xn[:, :, :], 0.0).then_inc(enc_in, 1)

            dve.wait_ge(dst_in, 16 * 6)
            dve.drain()
            for h in range(2):
                v.tensor_tensor(dst_d[:, h, :], dst_win[:, h, 1:], dst_win[:, h, 0:CH], ALU.not_equal)
            dve.drain()
            v.tensor_scalar(fall_sb[:, :, :], dst_d[:, :, :], FAR, None, ALU.mult).then_inc(fall_ready, 1)
            v.tensor_tensor(seam_fall[:, :], seam_dst[:, 0:1], seam_dst[:, 1:2], ALU.not_equal)
            dve.drain()
            v.tensor_scalar(seam_fall[:, :], seam_fall[:, :], FAR, None, ALU.mult)

            for j, (k0, w) in enumerate(GROUPS):
                dve.wait_ge(enc_mm, j + 1)
                last = v.tensor_copy(z[:, k0:k0 + w, :], pX[j % 2][0:NP, 0:w * H].rearrange("p (k c) -> p k c", c=H))
                last.then_inc(enc_out, 1)
            dve.wait_ge(enc_out, NG)
            dve.sem_inc(z_ready, 1)

            v.tensor_copy(dst_f[:, :], dst_cols[:, :])
            dve.drain()
            v.tensor_scalar(hi_f[:, :], dst_f[:, :], 1.0 / NK, -(NK // 2) / NK, ALU.mult, ALU.add)
            dve.drain()
            v.tensor_scalar(hi_f[:, :], hi_f[:, :], ROUND, None, ALU.add)
            dve.drain()
            v.tensor_scalar(hi_f[:, :], hi_f[:, :], -ROUND, None, ALU.add)
            dve.drain()
            v.tensor_copy(hi_b[:, :], hi_f[:, :])
            v.scalar_tensor_tensor(out=lo_b[:, :], in0=hi_f[:, :], scalar=-float(NK), in1=dst_f[:, :], op0=ALU.mult, op1=ALU.add)
            dve.drain()
            dve.sem_inc(hot_used, PRE)
            with dve.Fori(0, NHB // 2) as i:
                b = dve.snap(i * 2)
                for s in range(2):
                    dve.wait_ge(hot_used, done(b + (s - 2)))
                    cols = bass.ds((i * 2 + s) * HB, HB)
                    v.tensor_tensor(hot_hi[s][:, :, :], count_b[:, None, 0:NP].to_broadcast([NP, HB, NP]),
                                    hi_b[:, cols][:, :, None].to_broadcast([NP, HB, NP]), ALU.is_equal)
                    v.tensor_tensor(hot_lo[s][:, :, :], count_b[:, None, 0:NK].to_broadcast([NP, HB, NK]),
                                    lo_b[:, cols][:, :, None].to_broadcast([NP, HB, NK]), ALU.is_equal).then_inc(hot_ready, 1)
            dve.wait_ge(hist_done, 1)
            v.tensor_copy(hist[:, :], pT[0][0:NP, 0:NK])
            dve.drain()
            v.tensor_reduce(hist_sum[:, :], hist[:, :], AX.X, ALU.add).then_inc(cum_step, 1)
            v.memset(scr[:, :], 0.0)
            dve.drain()
            v.tensor_tensor_scan(cum[:, :], hist[:, :], scr[:, :], 0.0, ALU.add, ALU.add)
            v.tensor_scalar(has_edges[:, :], hist[:, :], 0.0, None, ALU.is_gt)
            dve.wait_ge(cum_mm, 1)
            dve.drain()
            v.tensor_scalar(cum[:, :], cum[:, :], pT[1][0:NP, 0:1], None, ALU.add)
            dve.drain()
            v.tensor_scalar(scr[:, :], cum[:, :], float(HALF_AT), 1e9, ALU.is_le, ALU.mult)
            dve.drain()
            v.tensor_tensor(scr[:, :], scr[:, :], cum[:, :], ALU.add)
            dve.drain()
            v.tensor_reduce(seam_col[:, :], scr[:, :], AX.X, ALU.min).then_inc(cum_step, 1)
            v.tensor_scalar(scr2[:, :], cum[:, :], -1.0, 0.0, ALU.add, ALU.max)
            dve.drain()
            v.tensor_scalar(scr[:, :], scr2[:, :], float(HALF_AT), float(SW_SHIFT), ALU.is_ge, ALU.mult)
            dve.drain()
            v.tensor_tensor(scr[:, :], scr[:, :], scr2[:, :], ALU.add)
            dve.drain()
            v.tensor_copy(row_idx[:, :], scr[:, :])
            dve.wait_ge(cum_mm, 2)
            v.tensor_reduce(seam_row[:, 0:1], pT[1][0:1, 0:NP], AX.X, ALU.min)
            dve.drain()
            v.tensor_scalar(seam_row[:, 1:2], seam_row[:, 0:1], -float(1 + HALF_AT), None, ALU.add)
            dve.drain()
            v.tensor_copy(seam_end[:, :], seam_row[:, 1:2]).then_inc(seam_known, 1)

            dve.wait_ge(par_in, 16 * N_PAR)
            for counter in (m_done, d_done, du_done, rex_done, sw_done, agg_done, mv1_done, y_hat_done, mv2_done):
                dve.sem_inc(counter, PRE)

            with dve.Fori(0, L) as l:
                one = bass.ds(l, 1)
                v.tensor_copy(t_now[:, :], t_all[:, one])
                v.tensor_copy(w1_now[:, :], w1b[:, one, :].rearrange("p o n -> p (o n)"))
                v.tensor_copy(w2_now[:, :], w2_all[:, one, :].rearrange("p o n -> p (o n)"))
                v.tensor_copy(g1_now[:, :], g1_all[:, one])
                v.tensor_copy(bb1_now[:, :], bb1_all[:, one])
                v.tensor_copy(b2_now[:, :], b2_all[:, one, :].rearrange("p o n -> p (o n)"))
                v.tensor_copy(lng_now[:, :], lng_all[:, one, :].rearrange("p o n -> p (o n)"))
                v.tensor_copy(lnb_now[:, :], lnb_all[:, one, :].rearrange("p o n -> p (o n)"))
                dve.drain().then_inc(layer_par, 1)

                def step(c, g, q, b=True, d=True):
                    s, s1 = c % 2, (c - 1) % 2
                    g_b, g_d = g + c, g + (c - 1)
                    if b:
                        dve.wait_ge(u_done, done(g_b))
                        dve.wait_ge(m_stored[s], (q + c // 2) * 16 + 16)
                        v.tensor_tensor_scan(M[s][:, 1:CH + 1], pR[s][:, :], du[s][:, 1, :], M[s1][:, CH:CH + 1], ALU.add, ALU.max)
                        v.tensor_copy(M[s][:, 0:1], M[s1][:, CH:CH + 1]).then_inc(m_done, 1)
                    if d:
                        dve.wait_ge(ex_done, done(g_d))
                        dve.wait_ge(sw_done, done(g_d - 1))
                        v.tensor_tensor(rex[:, :], r[s1][:, :], ex[s1][:, 1, :], ALU.mult).then_inc(rex_done, 1)
                    if b:
                        dve.wait_ge(m_done, done(g_b))
                        v.tensor_tensor(du[s][:, 0, :], pR[s][:, :], M[s][:, 0:CH], ALU.add).then_inc(d_done, 1)
                    if d:
                        dve.wait_ge(back_tp, 2 * g_d + (2 * PRE - 2))
                        v.tensor_tensor_scan(S[s1][:, :], ex[s1][:, 0, :], ex[s1][:, 1, :], S[s][:, CH - 1:CH], ALU.mult, ALU.add)
                    if b:
                        dve.wait_ge(d_done, done(g_b))
                        v.tensor_tensor(du[s][:, :, :], du[s][:, :, :], M[s][:, None, 1:CH + 1].to_broadcast([P, 2, CH]),
                                        ALU.subtract).then_inc(du_done, 1)
                    if d:
                        dve.wait_ge(rex_done, done(g_d))
                        v.tensor_tensor_scan(W[s1][:, :], ex[s1][:, 0, :], rex[:, :], W[s][:, CH - 1:CH], ALU.mult, ALU.add).then_inc(sw_done, 1)

                g0, q0 = dve.snap(l * NCH), dve.snap(l * (NCH // 2))
                step(0, g0, q0, d=False)
                step(1, g0, q0)
                with dve.Fori(1, NCH // 2 - 1) as i:
                    g, q = dve.snap(g0 + i * 2), dve.snap(q0 + i)
                    for c in range(2):
                        step(c, g, q)
                step(NCH - 2, g0, q0)
                step(NCH - 1, g0, q0)
                step(NCH, g0, q0, b=False)

                last_s = (NCH - 1) % 2
                dve.wait_ge(sw_done, g0 + (NCH + PRE))
                dve.wait_ge(seam_in, l * 32 + 32)
                v.tensor_tensor(seam_m[:, 0:1], M[last_s][0:H, CUT_COL + 1:CUT_COL + 2], seam_fall[:, :], ALU.add)
                dve.drain()
                v.tensor_tensor(seam_x[:, :], seam_m[:, 0:1], seam_m[:, 1:2], ALU.max)
                dve.drain()
                v.tensor_scalar(seam_m[:, :], seam_m[:, :], seam_x[:, :], None, ALU.subtract).then_inc(seam_max, 1)
                dve.wait_ge(seam_exp, l + 1)
                v.tensor_scalar(seam_sw1[:, :], seam_sw1[:, :], seam_e[:, 1:2], None, ALU.mult)
                dve.drain()
                for n, scanned in enumerate((S, W)):
                    v.scalar_tensor_tensor(out=seam_sw[:, n:n + 1], in0=scanned[last_s][0:H, CUT_COL:CUT_COL + 1],
                                           scalar=seam_e[:, 0:1], in1=seam_sw1[:, n:n + 1], op0=ALU.mult, op1=ALU.add)
                dve.drain().then_inc(seam_done, 1)

                G0 = dve.snap(l * NG)

                def aggregate(j):
                    k0, w = GROUPS[j]
                    ks = slice(k0, k0 + w)
                    dve.wait_ge(node_in[j], l * (16 * w) + 16 * w)
                    dve.wait_ge(node_tp, done(G0 + (j - 2)))
                    a = agg[j % 2][:, 0:w, :]
                    v.tensor_scalar(rden[:, 0:w, :], node_sw[:, ks, 0, :], DEN_EPS, None, ALU.add)
                    v.scalar_tensor_tensor(out=a, in0=node_sw[:, ks, 0, :], scalar=MSG_EPS, in1=node_sw[:, ks, 1, :], op0=ALU.mult, op1=ALU.add)
                    dve.drain()
                    v.reciprocal(rden[:, 0:w, :], rden[:, 0:w, :])
                    dve.drain()
                    v.tensor_tensor(a, a, rden[:, 0:w, :], ALU.mult)
                    dve.drain()
                    v.tensor_tensor(a, a, has_edges[:, ks][:, :, None].to_broadcast([NP, w, H]), ALU.mult)
                    dve.drain()
                    v.tensor_tensor(a, a, z[:, ks, :], ALU.add).then_inc(agg_done, 1)

                def norm1_stats(j):
                    w = GROUPS[j][1]
                    dve.wait_ge(y_mm, done(G0 + j))
                    for k in range(w):
                        v.bn_stats(stats[:, k, :], pX[j % 2][0:NP, k * H2:(k + 1) * H2])
                    dve.drain()
                    for k in range(w):
                        last = v.bn_aggr(mv1[j % 2][:, k, :], stats[:, k, :])
                    last.then_inc(mv1_done, 1)

                def norm1(j):
                    w = GROUPS[j][1]
                    dve.wait_ge(sd1_done, done(G0 + j))
                    dve.wait_ge(hat_tp, done(G0 + (j - 2)))
                    v.reciprocal(rs1[:, 0:w], sd1[j % 2][:, 0:w])
                    dve.drain()
                    for k in range(w):
                        last = v.tensor_scalar(y_hat[j % 2][:, k, :], pX[j % 2][0:NP, k * H2:(k + 1) * H2],
                                               mv1[j % 2][:, k, 0:1], rs1[:, k:k + 1], ALU.subtract, ALU.mult)
                    last.then_inc(y_hat_done, 1)

                def residual(j):
                    k0, w = GROUPS[j]
                    ks = slice(k0, k0 + w)
                    dve.wait_ge(o_mm, done(G0 + j))
                    v.tensor_tensor(hres[:, ks, :], hres[:, ks, :], b2_now[:, None, :].to_broadcast([NP, w, H]), ALU.add)
                    dve.drain()
                    v.tensor_tensor(hres[:, ks, :], pR[j % 2][0:NP, 0:w * H].rearrange("p (k c) -> p k c", c=H), hres[:, ks, :], ALU.add)
                    dve.drain()
                    for k in range(w):
                        v.bn_stats(stats2[:, k, :], hres[:, k0 + k, :])
                    dve.drain()
                    for k in range(w):
                        last = v.bn_aggr(mv2[j % 2][:, k, :], stats2[:, k, :])
                    last.then_inc(mv2_done, 1)

                def norm2(j):
                    k0, w = GROUPS[j]
                    ks = slice(k0, k0 + w)
                    dve.wait_ge(sd2_done, done(G0 + j))
                    v.reciprocal(rs2[:, 0:w], sd2[j % 2][:, 0:w])
                    dve.drain()
                    for k in range(w):
                        v.tensor_scalar(z[:, k0 + k, :], hres[:, k0 + k, :], mv2[j % 2][:, k, 0:1], rs2[:, k:k + 1],
                                        ALU.subtract, ALU.mult)
                    dve.drain()
                    v.tensor_tensor(z[:, ks, :], z[:, ks, :], lng_now[:, None, :].to_broadcast([NP, w, H]), ALU.mult)
                    dve.drain()
                    v.tensor_tensor(z[:, ks, :], z[:, ks, :], lnb_now[:, None, :].to_broadcast([NP, w, H]), ALU.add)
                    dve.drain()
                    v.tensor_scalar_max(z[:, ks, :], z[:, ks, :], 0.0)

                aggregate(0)
                for j in range(NG + 1):
                    if j + 1 < NG:
                        aggregate(j + 1)
                    if j < NG:
                        norm1_stats(j)
                    if j >= 1:
                        residual(j - 1)
                    if j < NG:
                        norm1(j)
                    if j >= 1:
                        norm2(j - 1)
                dve.drain().then_inc(z_ready, 1)

            v.tensor_tensor(x_in[:, :, :], x_in[:, :, :], z[:, :, :], ALU.add).then_inc(out_ready, 1)


_INS = ['x', 'src', 'dst', 'edge_attr_64', 'L0_gnn_enc_node_w', 'L0_gnn_enc_node_b', 'L0_gnn_enc_edge_w', 'L0_gnn_enc_edge_b',
        'L0_gnn_ln_g', 'L0_gnn_ln_b', 'L0_gnn_mlp1_w', 'L0_gnn_mlp1_b', 'L0_gnn_mlp_ln_g', 'L0_gnn_mlp_ln_b',
        'L0_gnn_mlp2_w', 'L0_gnn_mlp2_b', 'L0_gnn_t']


def kernel(**inputs):
    import numpy as _np
    import concourse.bacc as _bacc
    from concourse import mybir as _mybir
    from concourse.bass_utils import run_bass_kernel_spmd as _run

    nc = _bacc.Bacc("TRN2", target_bir_lowering=False, num_devices=1)
    arrays, args = {}, []
    for name in _INS:
        a = _np.ascontiguousarray(inputs[name])
        arrays[f"in_{name}_dram"] = a
        args.append(nc.dram_tensor(f"in_{name}_dram", a.shape, _mybir.dt.from_np(a.dtype), kind="ExternalInput").ap())
    args.append(nc.dram_tensor("out_0_dram", (N, H), _mybir.dt.float32, kind="ExternalOutput").ap())
    program(nc, *args)
    r = _run(nc, [arrays], core_ids=[0])
    return r.results[0]["out_0_dram"]
```

```python
import concourse.bass as bass
from concourse import mybir
from contextlib import ExitStack

F32 = mybir.dt.float32
BF16 = mybir.dt.bfloat16
I32 = mybir.dt.int32
U32 = mybir.dt.uint32
ALU = mybir.AluOpType
ACT = mybir.ActivationFunctionType
AX = mybir.AxisListType

N, H, E, L = 3125, 64, 100000, 4
H2 = 2 * H
MSG_EPS, DEN_EPS, LN_EPS = 1e-07, 1e-16, 1e-05
ROUND = 12582912.0
FAR = -1.0e30

P = 128
SUB = 4
CH = P * SUB
NCH = 98
HALF = NCH * CH
HALF_AT = E - HALF
assert HALF_AT <= HALF and NCH % 2 == 0
CUT_COL = (HALF_AT - 1) - (NCH - 1) * CH
assert 0 <= CUT_COL < CH
SW_SHIFT = HALF - HALF_AT

NP, NK = 125, 25
assert NP * NK == N
WIDTHS = (3, 4, 4, 4, 4, 4, 2)
GW = max(WIDTHS)
GROUPS = [(sum(WIDTHS[:j]), w) for j, w in enumerate(WIDTHS)]
assert sum(WIDTHS) == NK
NG = len(GROUPS)
ECOLS = E // NP
HB = 10
NHB = ECOLS // HB
assert NHB % 2 == 0 and NHB * HB == ECOLS and NHB <= NCH - 4
SB = 500
NSB = E // SB
assert NSB * SB == E
EMPTY_ROW = 2 * HALF
PRE = 2


def program(nc, x, src, dst, attr, enc_w, enc_b, edge_w, edge_b, ln_g, ln_b, w1, b1, g1, bb1, w2, b2, t, out):
    ctx = ExitStack()
    with ctx:
        ctx.enter_context(nc.allow_non_contiguous_dma(reason="columns of parameters"))

        def sb(name, shape, dt=F32):
            return ctx.enter_context(nc.sbuf_tensor(name, shape, dt))

        def pb(name, shape, dt=F32):
            return ctx.enter_context(nc.psum_tensor(name, shape, dt))

        def sem(name):
            return ctx.enter_context(nc.semaphore(name))

        z_rows = nc.dram_tensor("z_rows", (N, H), F32, kind="Internal").ap()
        sw_rows = nc.dram_tensor("sw_rows", (2 * HALF + 1, 2 * H), F32, kind="Internal").ap()
        max_cols = nc.dram_tensor("max_cols", (H, HALF), F32, kind="Internal").ap()
        fall_rows = nc.dram_tensor("fall_rows", (2, HALF), BF16, kind="Internal").ap()

        rank_of = nc.dram_tensor("rank_of", (E,), I32, kind="Internal").ap()
        src_sorted = nc.dram_tensor("src_sorted", (E, 1), I32, kind="Internal").ap()
        dst_sorted = nc.dram_tensor("dst_sorted", (E, 1), I32, kind="Internal").ap()
        attr_sorted = nc.dram_tensor("attr_sorted", (E, H), F32, kind="Internal").ap()

        ident = sb("ident", [P, P])
        half_sel = sb("half_sel", [2, P], BF16)
        below = sb("below", [NP, NP])
        edge_w2 = sb("edge_w2", [P, P])
        edge_b2 = sb("edge_b2", [P, 1])
        t_all = sb("t_all", [P, L])
        enc_wb = sb("enc_wb", [H + 1, H])
        w1b = sb("w1b", [H + 1, L, H2])
        w2_all = sb("w2_all", [H2, L, H])
        g1_all = sb("g1_all", [H2, L])
        bb1_all = sb("bb1_all", [H2, L])
        b2_all = sb("b2_all", [NP, L, H])
        zero_row = sb("zero_row", [1, 2 * H])
        lng_all = sb("lng_all", [NP, L, H])
        lnb_all = sb("lnb_all", [NP, L, H])
        t_now = sb("t_now", [P, 1])
        w1_now = sb("w1_now", [H + 1, H2])
        w2_now = sb("w2_now", [H2, H])
        g1_now = sb("g1_now", [H2, 1])
        bb1_now = sb("bb1_now", [H2, 1])
        lng_now = sb("lng_now", [NP, H])
        lnb_now = sb("lnb_now", [NP, H])

        idx_in = [sb(f"idx_in{s}", [P, 2, SUB], I32) for s in range(2)]
        row_idx = sb("row_idx", [NP, NK], I32)
        has_edges = sb("has_edges", [NP, NK])
        seam_end = sb("seam_end", [1, 1], I32)
        seam_fall = sb("seam_fall", [H, 1])

        def two(name, shape, dt=F32):
            return [sb(f"{name}{s}", shape, dt) for s in range(2)]

        attr_in = two("attr_in", [P, SUB, 2, H])
        fall_in = two("fall_in", [2, CH], BF16)
        zsrc = two("zsrc", [P, SUB, 2, H])
        attr_t = two("attr_t", [P, CH])
        r = two("r", [P, CH])
        du = two("du", [P, 2, CH])
        ex = two("ex", [P, 2, CH])
        rex = sb("rex", [P, CH])
        M = two("M", [P, CH + 1])
        S = two("S", [P, CH])
        W = two("W", [P, CH])
        sw_out = two("sw_out", [P, 2, SUB, 2, H])

        seam_m = sb("seam_m", [H, 2])
        seam_x = sb("seam_x", [H, 1])
        seam_e = sb("seam_e", [H, 2])
        seam_sw1 = sb("seam_sw1", [H, 2])
        seam_sw = sb("seam_sw", [H, 2])

        node_sw = sb("node_sw", [NP, NK, 2, H])
        z = sb("z", [NP, NK, H])
        hres = sb("hres", [NP, NK, H])
        x_in = sb("x_in", [NP, NK, H])
        agg = two("agg", [NP, GW, H])
        rden = sb("rden", [NP, GW, H])
        node_t = two("node_t", [H + 1, GW * NP])
        sq1, sum1, sd1 = two("sq1_", [NP, GW, H2]), two("sum1_", [NP, GW]), two("sd1_", [NP, GW])
        rs1 = two("rs1_", [NP, GW])
        y_hat = two("y_hat", [NP, GW, H2])
        hid_t = two("hid_t", [H2, GW * NP])
        sq2, sum2, sd2 = two("sq2_", [NP, GW, H]), two("sum2_", [NP, GW]), two("sd2_", [NP, GW])
        rs2 = two("rs2_", [NP, GW])
        w1_mean = sb("w1_mean", [H + 1, L])
        w2_mean = sb("w2_mean", [H2, L])
        b2_mean = sb("b2_mean", [NP, L])
        eps_col = sb("eps_col", [P, 1])

        dst_win = sb("dst_win", [NCH, 2, CH + 1], I32)
        fall_sb = sb("fall_sb", [NCH, 2, CH], BF16)
        dst_cols = sb("dst_cols", [NP, ECOLS], I32)
        dst_f = sb("dst_f", [NP, ECOLS])
        hi_f = sb("hi_f", [NP, ECOLS])
        hi_b = sb("hi_b", [NP, ECOLS], BF16)
        lo_b = sb("lo_b", [NP, ECOLS], BF16)
        count_i = sb("count_i", [NP, NP], I32)
        count_b = sb("count_b", [NP, NP], BF16)
        hot_hi = two("hot_hi", [NP, HB, NP], BF16)
        hot_lo = two("hot_lo", [NP, HB, NK], BF16)
        hist = sb("hist", [NP, NK])
        hist_sum = sb("hist_sum", [NP, 1])
        cum = sb("cum", [NP, NK])
        scr = sb("scr", [NP, NK])
        scr2 = sb("scr2", [NP, NK])
        seam_col = sb("seam_col", [NP, 1])
        seam_row = sb("seam_row", [1, 4])
        seam_dst = sb("seam_dst", [H, 2], I32)
        drops = sb("drops", [NCH, 2, CH])
        drop_col = sb("drop_col", [NCH, 1])
        drop_flag = sb("drop_flag", [1, 1])
        unsorted_i = sb("unsorted_i", [1, 1], I32)
        node_i = sb("node_i", [NP, NK], I32)
        node_f = sb("node_f", [NP, NK])
        dst_all = sb("dst_all", [NP, SB], I32)
        dst_all_f = sb("dst_all_f", [NP, SB])
        is_node = sb("is_node", [NP, SB])
        nth = sb("nth", [NP, SB])
        rank_part = sb("rank_part", [NP, SB])
        no_add = sb("no_add", [NP, SB])
        ones_col = sb("ones_col", [NP, 1])
        block_count = sb("block_count", [NP, NK])
        next_rank = sb("next_rank", [NP, NK])
        row_count = sb("row_count", [NP, 1])
        rank_row = sb("rank_row", [1, SB], I32)
        rank_cols = sb("rank_cols", [NP, ECOLS], I32)
        src_cols = sb("src_cols", [NP, ECOLS], I32)
        move_attr = sb("move_attr", [NP, H])
        move_rank = sb("move_rank", [NP, 1], I32)
        move_src = sb("move_src", [NP, 1], I32)
        move_dst = sb("move_dst", [NP, 1], I32)
        zeros_b = sb("zeros_b", [NP, NP], BF16)
        xn = sb("xn", [NP, NK, H])
        stats_all = sb("stats_all", [NP, NK, 6])
        mv_all = sb("mv_all", [NP, NK, 2])
        dst_d = sb("dst_d", [NCH, 2, CH])

        pA = pb("pA", [P, CH])
        pH = pb("pH", [P, CH])
        pX = [pb(f"pX{s}", [P, CH]) for s in range(2)]
        pR = [pb(f"pR{s}", [P, CH]) for s in range(2)]
        pT = [pb(f"pT{s}", [P, CH]) for s in range(2)]

        par_in = sem("par_in")
        dst_in = sem("dst_in")
        x_loaded = sem("x_loaded")
        consts = sem("consts")
        dve_consts = sem("dve_consts")
        fall_ready, fall_stored = sem("fall_ready"), sem("fall_stored")
        hot_ready, hot_used, hist_done, cum_step, cum_mm = (sem(n) for n in ("hot_ready", "hot_used", "hist_done", "cum_step", "cum_mm"))
        seam_known = sem("seam_known")
        order_step, order_tp, order_known = sem("order_step"), sem("order_tp"), sem("order_known")
        block_in, block_seen, rank_summed, rank_mm, rank_ready, rank_stored, rank_base, rank_base_mm = (
            sem(n) for n in ("block_in", "block_seen", "rank_summed", "rank_mm", "rank_ready", "rank_stored", "rank_base", "rank_base_mm"))
        cols_in, move_in, move_ready, moved, move_free, resorted_in = (
            sem(n) for n in ("cols_in", "move_in", "move_ready", "moved", "move_free", "resorted_in"))
        enc_in, enc_tp, enc_sb, enc_mm, enc_out = (sem(n) for n in ("enc_in", "enc_tp", "enc_sb", "enc_mm", "enc_out"))
        z_ready, z_stored = sem("z_ready"), sem("z_stored")
        layer_par = sem("layer_par")
        idx_loaded = [sem(f"idx_loaded{s}") for s in range(2)]
        loads = [sem(f"loads{s}") for s in range(2)]
        gathered = [sem(f"gathered{s}") for s in range(2)]
        m_stored = [sem(f"m_stored{s}") for s in range(2)]
        sw_stored = [sem(f"sw_stored{s}") for s in range(2)]
        attr_tp = sem("attr_tp")
        attr_sb = sem("attr_sb")
        x_mm = sem("x_mm")
        r_done = sem("r_done")
        u_done = sem("u_done")
        m_done = sem("m_done")
        d_done = sem("d_done")
        du_done = sem("du_done")
        ex_done = sem("ex_done")
        rex_done = sem("rex_done")
        sw_done = sem("sw_done")
        back_tp = sem("back_tp")
        back_sb = sem("back_sb")
        seam_in, seam_max, seam_exp, seam_done, seam_stored = (sem(n) for n in ("seam_in", "seam_max", "seam_exp", "seam_done", "seam_stored"))
        node_in = [sem(f"node_in{j}") for j in range(NG)]
        agg_done = sem("agg_done")
        node_tp = sem("node_tp")
        node_t_sb = sem("node_t_sb")
        y_mm = sem("y_mm")
        sd1_done = sem("sd1_done")
        y_hat_done = sem("y_hat_done")
        hat_tp = sem("hat_tp")
        hid_done = sem("hid_done")
        o_mm = sem("o_mm")
        hres_done = sem("hres_done")
        sd2_done = sem("sd2_done")
        sum1_done, sum2_done = sem("sum1_done"), sem("sum2_done")
        out_ready, out_stored = sem("out_ready"), sem("out_stored")

        sp_passed, pool_passed, pe_passed = (sem(f"{n}_passed") for n in ("sp", "pool", "pe"))

        N_PAR = 2 + 9 + 4 + 2

        def done(turn):
            return turn + (1 + PRE)

        def value(engine, v):
            return v if isinstance(v, int) else engine.snap(v)

        def edge_rows(ap, h, first):
            return ap[bass.ds(first, CH), :].rearrange("(p t) c -> p t c", t=SUB)

        block = ctx.enter_context(nc.Block())

        @block.sync
        def _(sp):
            sp.dma_start(x_in[:, :, :], x.rearrange("(p k) c -> p k c", k=NK)).then_inc(x_loaded, 16)
            def load_windows(table, signal):
                for h in range(2):
                    first = h * HALF_AT
                    sp.dma_start(dst_win[:, h, 1:], table[first:first + HALF].rearrange("(q j) -> q j", j=CH)).then_inc(signal, 16)
                    tail = table[first:first + HALF - CH].rearrange("(q j) -> q j", j=CH)
                    sp.dma_start(dst_win[1:NCH, h, 0:1], tail[:, CH - 1:CH]).then_inc(signal, 16)
                sp.dma_start(seam_dst[:, :], table[HALF_AT - 1:HALF_AT + 1][None, :].to_broadcast([H, 2])).then_inc(signal, 16)

            load_windows(dst, dst_in)
            sp.dma_start(dst_cols[:, :], dst.rearrange("(p c) -> p c", c=ECOLS)).then_inc(cols_in, 16)

            sp.wait_ge(order_known, 1)
            unsorted = sp.value_load(unsorted_i[0:1, 0:1], min_val=0, max_val=1)
            with sp.If(unsorted != 0):
                sp.sem_inc(rank_stored, 16)
                for sweep in range(2):
                    with sp.Fori(0, NSB) as b:
                        turn = sp.snap(b + sweep * NSB)
                        sp.wait_ge(block_seen, turn + 1)
                        sp.sem_inc(sp_passed, 1)
                        sp.dma_start(dst_all[:, :], dst[bass.ds(b * SB, SB)][None, :].to_broadcast([NP, SB])).then_inc(block_in, 16)
                        if sweep:
                            sp.wait_ge(rank_ready, b + 1)
                            sp.sem_inc(sp_passed, 1)
                            sp.dma_start(rank_of[bass.ds(b * SB, SB)][None, :], rank_row[:, :]).then_inc(rank_stored, 16)
                sp.wait_ge(rank_stored, 16 * (NSB + 1))
                sp.dma_start(rank_cols[:, :], rank_of.rearrange("(p c) -> p c", c=ECOLS)).then_inc(cols_in, 16)
                sp.dma_start(src_cols[:, :], src.rearrange("(p c) -> p c", c=ECOLS)).then_inc(cols_in, 16)
                with sp.Fori(0, ECOLS) as c:
                    sp.wait_ge(move_free, c + 1)
                    sp.sem_inc(sp_passed, 1)
                    sp.dma_start(move_attr[:, :], attr.rearrange("(p c) h -> p c h", c=ECOLS)[:, bass.ds(c, 1), :].rearrange("p o h -> p (o h)")).then_inc(move_in, 16)
                sp.wait_ge(move_free, ECOLS + 1)
                load_windows(dst_sorted.rearrange("e o -> (e o)"), resorted_in)

            def load(first_edge, s):
                with sp.If(unsorted != 0):
                    for h in range(2):
                        sp.dma_start(attr_in[s][:, :, h, :], edge_rows(attr_sorted, h, first_edge + h * HALF_AT)).then_inc(loads[s], 16)
                with sp.Else():
                    for h in range(2):
                        sp.dma_start(attr_in[s][:, :, h, :], edge_rows(attr, h, first_edge + h * HALF_AT)).then_inc(loads[s], 16)
                sp.dma_start(fall_in[s][:, :], fall_rows[:, bass.ds(first_edge, CH)]).then_inc(loads[s], 16)

            def load_idx(first_edge, s):
                def load_from(table):
                    for h in range(2):
                        sp.dma_start(idx_in[s][:, h, :], table[bass.ds(first_edge + h * HALF_AT, CH)].rearrange("(p t) -> p t", t=SUB)).then_inc(idx_loaded[s], 16)

                with sp.If(unsorted != 0):
                    load_from(src_sorted.rearrange("e o -> (e o)"))
                with sp.Else():
                    load_from(src)

            def store_m(first_edge, s, g):
                sp.wait_ge(m_done, done(g))
                sp.sem_inc(sp_passed, 1)
                sp.dma_start(max_cols[:, bass.ds(first_edge, CH)], M[s][H:P, 1:CH + 1]).then_inc(m_stored[s], 16)

            def store_sw(first_edge, s, g):
                sp.wait_ge(back_sb, 2 * g + 2 * (1 + PRE))
                for h in range(2):
                    sp.dma_start(edge_rows(sw_rows, h, first_edge + h * HALF).rearrange("p t c -> p (t c)"),
                                 sw_out[s][:, h, :, :, :].rearrange("p t s c -> p (t s c)")).then_inc(sw_stored[s], 16)

            for s in range(2):
                sp.sem_inc(m_stored[s], 16)
                sp.sem_inc(sw_stored[s], 32)
                load_idx(s * CH, s)

            sp.wait_ge(z_ready, 1)
            sp.dma_start(z_rows.rearrange("(p k) c -> p k c", k=NK), z[:, :, :]).then_inc(z_stored, 16)
            sp.wait_ge(fall_ready, 1)
            for h in range(2):
                sp.dma_start(fall_rows[h, :].rearrange("(q j) -> q j", j=CH), fall_sb[:, h, :]).then_inc(fall_stored, 16)
            sp.dma_start(sw_rows[EMPTY_ROW:EMPTY_ROW + 1, :], zero_row[:, :]).then_inc(fall_stored, 16)
            sp.wait_ge(fall_stored, 48)
            for s in range(2):
                load(s * CH, s)

            def layer(l, seam_at):
                def step(first, g, q, s, load_at=None, sw=True):
                    at = first + 2 * CH if load_at is None else load_at
                    sp.wait_ge(gathered[s], q * 128 + 128)
                    sp.sem_inc(sp_passed, 1)
                    load_idx(at, s)
                    sp.wait_ge(attr_tp, done(g))
                    sp.sem_inc(sp_passed, 1)
                    load(at, s)
                    store_m(first, s, g)
                    if sw:
                        store_sw(first - 3 * CH, 1 - s, g - 3)

                g0, q0 = value(sp, l * NCH), value(sp, l * (NCH // 2))
                for c in range(4):
                    step(c * CH, g0 + c, q0 + c // 2, c % 2, sw=c >= 3)
                with sp.Fori(2, NCH // 2 - 1) as i:
                    first, g, q = sp.snap(i * (2 * CH)), sp.snap(g0 + i * 2), sp.snap(q0 + i)
                    for s in range(2):
                        step(first + s * CH, g + s, q, s)
                for c in range(NCH - 2, NCH):
                    step(c * CH, g0 + c, q0 + c // 2, c % 2, load_at=(c % 2) * CH)
                for c in range(NCH - 3, NCH):
                    store_sw(c * CH, c % 2, g0 + c)
                if seam_at is None:
                    sp.wait_ge(seam_known, 1)
                    seam_at = sp.value_load(seam_end[0:1, 0:1], min_val=0, max_val=HALF - 1)
                q = value(sp, l * (NCH // 2))
                for s in range(2):
                    sp.wait_ge(sw_stored[s], q * 32 + 32 * (NCH // 2 + 1))
                    sp.wait_ge(m_stored[s], q * 16 + 16 * (NCH // 2 + 1))
                sp.sem_inc(sp_passed, 1)
                sp.dma_start(seam_m[:, 1:2], max_cols[:, bass.ds(seam_at, 1)]).then_inc(seam_in, 16)
                seam_row_ap = sw_rows[bass.ds(seam_at + HALF, 1), :].rearrange("o (s c) -> c (o s)", s=2)
                sp.dma_start(seam_sw1[:, :], seam_row_ap).then_inc(seam_in, 16)
                sp.wait_ge(seam_done, l + 1)
                sp.dma_start(sw_rows[bass.ds(seam_at + HALF, 1), :].rearrange("o (s c) -> c (o s)", s=2),
                             seam_sw[:, :]).then_inc(seam_stored, 16)
                sp.wait_ge(z_ready, l + 2)
                sp.dma_start(z_rows.rearrange("(p k) c -> p k c", k=NK), z[:, :, :]).then_inc(z_stored, 16)
                return seam_at

            seam_at = layer(0, None)
            with sp.Fori(1, L) as l:
                layer(l, seam_at)
            sp.wait_ge(z_stored, 16 * (L + 1))
            sp.wait_ge(out_ready, 1)
            sp.dma_start(out.rearrange("(p k) c -> p k c", k=NK), x_in[:, :, :]).then_inc(out_stored, 16)
            for s in range(2):
                sp.wait_ge(loads[s], 48 * (L * NCH // 2 + 1))
                sp.wait_ge(idx_loaded[s], 32 * (L * NCH // 2 + 1))
            sp.wait_ge(out_stored, 16)

        @block.gpsimd
        def _(pool):
            pool.memset(ident[:, :], 0.0).then_inc(consts, 1)
            pool.memset(below[:, :], 0.0).then_inc(consts, 1)
            pool.memset(half_sel[:, :], 0.0).then_inc(consts, 1)
            pool.wait_ge(consts, 3)
            pool.affine_select(out=ident[:, :], in_=ident[:, :], compare_op=ALU.not_equal, fill=1.0, base=0,
                               pattern=[[-1, P]], channel_multiplier=1).then_inc(consts, 1)
            pool.affine_select(out=below[:, :], in_=below[:, :], compare_op=ALU.is_ge, fill=1.0, base=0,
                               pattern=[[-1, NP]], channel_multiplier=1).then_inc(consts, 1)
            pool.affine_select(out=half_sel[:, :].rearrange("p (m c) -> p m c", c=H),
                               in_=half_sel[:, :].rearrange("p (m c) -> p m c", c=H), compare_op=ALU.not_equal,
                               fill=1.0, base=0, pattern=[[-1, 2], [0, H]], channel_multiplier=1).then_inc(consts, 1)
            pool.iota(node_i[:, :], pattern=[[1, NK]], base=0, channel_multiplier=NK).then_inc(consts, 1)
            pool.iota(count_i[:, :], pattern=[[1, NP]], base=0, channel_multiplier=0).then_inc(consts, 1)
            pool.wait_ge(order_known, 1)
            unsorted = pool.value_load(unsorted_i[0:1, 0:1], min_val=0, max_val=1)
            with pool.If(unsorted != 0):
                pool.sem_inc(move_free, 1)
                with pool.Fori(0, ECOLS) as c:
                    pool.wait_ge(move_in, c * 16 + 16)
                    pool.wait_ge(move_ready, c + 1)
                    pool.sem_inc(pool_passed, 1)
                    for table, rows in ((attr_sorted, move_attr), (src_sorted, move_src), (dst_sorted, move_dst)):
                        pool.indirect_dma_start(table, bass.IndirectOffsetOnAxis(move_rank[:, :].bitcast(U32), 0),
                                                rows[:, :], None).then_inc(moved, 16)
                    pool.wait_ge(moved, c * 48 + 48)
                    pool.sem_inc(move_free, 1)

            def layer(l):
                pool.wait_ge(z_stored, l * 16 + 16)
                pool.sem_inc(pool_passed, 1)
                with pool.Fori(0, NCH // 2) as i:
                    g, q = pool.snap(l * NCH + i * 2), pool.snap(l * (NCH // 2) + i)
                    for s in range(2):
                        pool.wait_ge(x_mm, done(g + (s - 2)))
                        pool.wait_ge(idx_loaded[s], q * 32 + 32)
                        pool.sem_inc(pool_passed, 1)
                        for h in range(2):
                            for t4 in range(SUB):
                                pool.indirect_dma_start(
                                    zsrc[s][:, t4, h, :], None, z_rows,
                                    bass.IndirectOffsetOnAxis(idx_in[s][:, h, t4:t4 + 1].bitcast(U32), 0)).then_inc(gathered[s], 16)
                pool.wait_ge(seam_stored, l * 16 + 16)
                pool.sem_inc(pool_passed, 1)
                for j, (k0, w) in enumerate(GROUPS):
                    for k in range(k0, k0 + w):
                        pool.indirect_dma_start(
                            node_sw[:, k, :, :].rearrange("p s c -> p (s c)"), None, sw_rows,
                            bass.IndirectOffsetOnAxis(row_idx[:, k:k + 1].bitcast(U32), 0)).then_inc(node_in[j], 16)

            layer(0)
            with pool.Fori(1, L) as l:
                layer(l)

        @block.scalar
        def _(act):
            for h in range(2):
                rows = slice(h * H, h * H + H)
                act.dma_start(edge_b2[rows, :], edge_b[:, None]).then_inc(par_in, 16)
            act.dma_start(t_all[:, :], t[None, :].to_broadcast([P, L])).then_inc(par_in, 16)
            act.dma_start(enc_wb[0:H, :], enc_w).then_inc(par_in, 16)
            act.dma_start(enc_wb[H:H + 1, :], enc_b[None, :]).then_inc(par_in, 16)
            act.dma_start(w1b[0:H, :, :], w1.rearrange("l c n -> c l n")).then_inc(par_in, 16)
            act.dma_start(w1b[H:H + 1, :, :], b1[None, :, :]).then_inc(par_in, 16)
            act.dma_start(w2_all[:, :, :], w2.rearrange("l c n -> c l n")).then_inc(par_in, 16)
            act.dma_start(g1_all[:, :], g1.rearrange("l c -> c l")).then_inc(par_in, 16)
            act.dma_start(bb1_all[:, :], bb1.rearrange("l c -> c l")).then_inc(par_in, 16)
            for all_, dram in ((lng_all, ln_g), (lnb_all, ln_b)):
                act.dma_start(all_[:, 0:L - 1, :], dram[None, 1:L, :].to_broadcast([NP, L - 1, H])).then_inc(par_in, 16)
                act.dma_start(all_[:, L - 1:L, :], dram[None, 0:1, :].to_broadcast([NP, 1, H])).then_inc(par_in, 16)
            act.dma_start(b2_all[:, :, :], b2[None, :, :].to_broadcast([NP, L, H])).then_inc(par_in, 16)
            act.wait_ge(dve_consts, 1)
            for h in range(2):
                rows = slice(h * H, h * H + H)
                act.dma_start(edge_w2[rows, rows], edge_w).then_inc(par_in, 16)

            act.wait_ge(enc_in, 1)
            act.activation(scr2[:, :], scr[:, :], ACT.Sqrt, bias=eps_col[0:NP, :]).then_inc(enc_in, 1)
            for j, (k0, w) in enumerate(GROUPS):
                act.wait_ge(enc_tp, j + 1)
                if j >= 2:
                    act.wait_ge(enc_mm, j - 1)
                act.activation(node_t[j % 2][0:H, 0:w * NP], (pA, pH)[j % 2][0:H, 0:w * NP], ACT.Copy).then_inc(enc_sb, 1)

            act.sem_inc(attr_sb, PRE)
            act.sem_inc(r_done, PRE)
            act.sem_inc(u_done, PRE)
            act.sem_inc(ex_done, PRE)
            act.sem_inc(back_sb, 2 * PRE)
            act.sem_inc(node_t_sb, PRE)
            act.sem_inc(sd1_done, PRE)
            act.sem_inc(hid_done, PRE)
            act.sem_inc(sd2_done, PRE)

            def layer(l):
                act.wait_ge(layer_par, l + 1)

                def messages(s, g):
                    act.wait_ge(attr_tp, done(g))
                    act.activation(attr_t[s][:, :], pA[:, :], ACT.Copy).then_inc(attr_sb, 1)
                    act.wait_ge(x_mm, done(g))
                    act.wait_ge(rex_done, done(g - 2))
                    act.activation(r[s][:, :], pX[s][:, :], ACT.Relu, bias=edge_b2[:, :]).then_inc(r_done, 1)
                    act.wait_ge(r_done, done(g))
                    act.activation(du[s][:, 1, :], r[s][:, :], ACT.Copy, scale=t_now[:, 0:1]).then_inc(u_done, 1)

                def exps(s, g):
                    act.wait_ge(du_done, done(g))
                    act.activation(ex[s][:, :, :], du[s][:, :, :], ACT.Exp).then_inc(ex_done, 1)

                def copy_out(s, g, q):
                    act.wait_ge(sw_stored[s], q * 32 + 32)
                    for b in range(2):
                        act.wait_ge(back_tp, 2 * g + (2 * PRE + b + 1))
                        act.activation(sw_out[s][:, :, 2 * b:2 * b + 2, :, :].rearrange("p h t s c -> p (t s) h c"),
                                       pT[b][:, :].rearrange("p (a h c) -> p a h c", a=4, h=2), ACT.Copy).then_inc(back_sb, 1)

                def step(c, g, q, a=True, e=True, o=True):
                    if a:
                        messages((c + 1) % 2, g + (c + 1))
                    if o:
                        copy_out(c % 2, g + (c - 2), q + (c - 2) // 2)
                    if e:
                        exps(c % 2, g + c)

                g0, q0 = value(act, l * NCH), value(act, l * (NCH // 2))
                step(-1, g0, q0, e=False, o=False)
                for c in range(2):
                    step(c, g0, q0, o=False)
                with act.Fori(1, NCH // 2 - 1) as i:
                    g, q = act.snap(g0 + i * 2), act.snap(q0 + i)
                    for c in range(2):
                        step(c, g, q)
                step(NCH - 2, g0, q0)
                step(NCH - 1, g0, q0, a=False)
                step(NCH, g0, q0, a=False, e=False)
                step(NCH + 1, g0, q0, a=False, e=False)

                act.wait_ge(seam_max, l + 1)
                act.activation(seam_e[:, :], seam_m[:, :], ACT.Exp).then_inc(seam_exp, 1)

                G0 = value(act, l * NG)

                def to_sb(j):
                    act.wait_ge(node_tp, done(G0 + j))
                    act.wait_ge(y_mm, done(G0 + (j - 2)))
                    w = GROUPS[j][1]
                    act.activation(node_t[j % 2][0:H, 0:w * NP], (pA, pH)[j % 2][0:H, 0:w * NP], ACT.Copy).then_inc(node_t_sb, 1)

                def deviation1(j):
                    act.wait_ge(y_mm, done(G0 + j))
                    w = GROUPS[j][1]
                    for k in range(w):
                        last = act.activation(sq1[j % 2][:, k, :], pX[j % 2][0:NP, k * H2:(k + 1) * H2], ACT.Square,
                                              accum_out=sum1[j % 2][:, k:k + 1])
                    last.then_inc(sum1_done, 1)
                    act.wait_ge(sum1_done, G0 + (j + 1))
                    act.activation(sd1[j % 2][:, 0:w], sum1[j % 2][:, 0:w], ACT.Sqrt, bias=eps_col[0:NP, :],
                                   scale=1.0 / H2).then_inc(sd1_done, 1)

                def deviation2(j):
                    act.wait_ge(hres_done, done(G0 + j))
                    k0, w = GROUPS[j]
                    for k in range(w):
                        last = act.activation(sq2[j % 2][:, k, :], hres[:, k0 + k, :], ACT.Square,
                                              accum_out=sum2[j % 2][:, k:k + 1])
                    last.then_inc(sum2_done, 1)
                    act.wait_ge(sum2_done, G0 + (j + 1))
                    act.activation(sd2[j % 2][:, 0:w], sum2[j % 2][:, 0:w], ACT.Sqrt, bias=eps_col[0:NP, :],
                                   scale=1.0 / H).then_inc(sd2_done, 1)

                def hidden(j):
                    act.wait_ge(hat_tp, done(G0 + j))
                    act.wait_ge(o_mm, done(G0 + (j - 2)))
                    w = GROUPS[j][1]
                    act.activation(hid_t[j % 2][:, 0:w * NP], pT[j % 2][:, 0:w * NP], ACT.Relu,
                                   bias=bb1_now[:, :], scale=g1_now[:, :]).then_inc(hid_done, 1)

                to_sb(0)
                deviation1(0)
                to_sb(1)
                for j in range(NG + 1):
                    if j < NG:
                        hidden(j)
                    if j + 1 < NG:
                        deviation1(j + 1)
                    if j + 2 < NG:
                        to_sb(j + 2)
                    if j >= 1:
                        deviation2(j - 1)

            layer(0)
            with act.Fori(1, L) as l:
                layer(l)

        @block.tensor
        def _(pe):
            pe.wait_ge(consts, 8)
            pe.wait_ge(dve_consts, 5)
            pe.wait_ge(par_in, 16 * N_PAR)
            for j, (k0, w) in enumerate(GROUPS):
                pe.wait_ge(enc_in, 3)
                if j >= 2:
                    pe.wait_ge(enc_sb, j - 1)
                for k in range(w):
                    last = pe.transpose((pA, pH)[j % 2][0:H, k * NP:(k + 1) * NP], xn[:, k0 + k, :], ident[0:NP, 0:NP])
                last.then_inc(enc_tp, 1)
                pe.wait_ge(enc_sb, j + 1)
                if j >= 2:
                    pe.wait_ge(enc_out, j - 1)
                for k in range(w):
                    last = pe.matmul(pX[j % 2][0:NP, k * H:(k + 1) * H], node_t[j % 2][:, k * NP:(k + 1) * NP],
                                     enc_wb[:, :], start=True, stop=True)
                last.then_inc(enc_mm, 1)
                if j == 0:
                    pe.wait_ge(order_step, 1)
                    pe.transpose(pT[0][0:1, 0:NCH], drop_col[:, :], ident[0:NCH, 0:NCH]).then_inc(order_tp, 1)
            pe.wait_ge(order_known, 1)
            unsorted = pe.value_load(unsorted_i[0:1, 0:1], min_val=0, max_val=1)
            with pe.If(unsorted != 0):
                pe.wait_ge(rank_base, 1)
                pe.matmul(pH[0:NP, 0:1], below[:, :], row_count[:, :], start=True, stop=True).then_inc(rank_base_mm, 1)
                with pe.Fori(0, NSB) as b:
                    pe.wait_ge(rank_summed, b + 1)
                    pe.matmul(pT[0][0:1, 0:SB], ones_col[:, :], rank_part[:, :], start=True, stop=True).then_inc(rank_mm, 1)

            pe.sem_inc(attr_tp, PRE)
            pe.sem_inc(x_mm, PRE)
            pe.sem_inc(back_tp, 2 * PRE)
            pe.sem_inc(node_tp, PRE)
            pe.sem_inc(y_mm, PRE)
            pe.sem_inc(hat_tp, PRE)
            pe.sem_inc(o_mm, PRE)

            def layer(l, first_layer=False):
                pe.wait_ge(z_ready, l + 1)

                def front(s, g, q):
                    pe.wait_ge(loads[s], q * 48 + 48)
                    pe.wait_ge(d_done, done(g - 2))
                    pe.matmul(pR[s][:, :], half_sel[:, :], fall_in[s][:, :], start=True, stop=True)
                    for t4 in range(SUB):
                        last = pe.transpose(pA[:, t4:CH:SUB], attr_in[s][:, t4, :, :].rearrange("p h c -> p (h c)"), ident[:, :])
                    last.then_inc(attr_tp, 1)
                    pe.wait_ge(attr_sb, done(g))
                    pe.matmul(pX[s][:, :], edge_w2[:, :], attr_t[s][:, :], start=True, stop=False, skip_group_check=True)
                    pe.wait_ge(gathered[s], q * 128 + 128)
                    for t4 in range(SUB):
                        last = pe.matmul(pX[s][:, t4:CH:SUB], zsrc[s][:, t4, :, :].rearrange("p h c -> p (h c)"), ident[:, :],
                                         start=False, stop=(t4 == SUB - 1), skip_group_check=True)
                    last.then_inc(x_mm, 1)

                def back(s, g):
                    pe.wait_ge(sw_done, done(g))
                    for b in range(2):
                        pe.wait_ge(back_sb, 2 * g + (2 * PRE + b - 1))
                        for t4 in range(2 * b, 2 * b + 2):
                            for n, scanned in enumerate((S, W)):
                                at = ((t4 % 2) * 2 + n) * P
                                last = pe.transpose(pT[b][:, at:at + P], scanned[s][:, t4:CH:SUB], ident[:, :])
                        last.then_inc(back_tp, 1)

                def step(c, g, q, a=True, o=True):
                    if a:
                        front((c + 1) % 2, g + (c + 1), q + (c + 1) // 2)
                    if o:
                        back(c % 2, g + (c - 2))

                g0, q0 = value(pe, l * NCH), value(pe, l * (NCH // 2))
                for c in range(-1, 2):
                    step(c, g0, q0, o=False)
                i0 = 1
                if first_layer:
                    hist_mm = dict(skip_group_check=True)
                    pe.matmul(pH[0:NP, 0:NK], zeros_b[:, :], zeros_b[:, 0:NK], start=True, stop=False, **hist_mm)
                    i0 += NHB // 2
                    with pe.Fori(1, i0) as i:
                        g, q = pe.snap(g0 + i * 2), pe.snap(q0 + i)
                        for c in range(2):
                            step(c, g, q)
                            pe.wait_ge(hot_ready, i * 2 + (c - 1))
                            for col in range(HB):
                                last = pe.matmul(pH[0:NP, 0:NK], hot_hi[c][:, col, :], hot_lo[c][:, col, :],
                                                 start=False, stop=False, **hist_mm)
                            last.then_inc(hot_used, 1)
                    pe.matmul(pH[0:NP, 0:NK], zeros_b[:, :], zeros_b[:, 0:NK], start=False, stop=True,
                              **hist_mm).then_inc(hist_done, 1)
                    pe.wait_ge(cum_step, 1)
                    pe.matmul(pH[0:NP, 64:65], below[:, :], hist_sum[:, :], start=True, stop=True).then_inc(cum_mm, 1)
                    pe.wait_ge(cum_step, 2)
                    pe.transpose(pH[0:1, 128:128 + NP], seam_col[:, :], ident[0:NP, 0:NP]).then_inc(cum_mm, 1)
                with pe.Fori(i0, NCH // 2 - 1) as i:
                    g, q = pe.snap(g0 + i * 2), pe.snap(q0 + i)
                    for c in range(2):
                        step(c, g, q)
                step(NCH - 2, g0, q0)
                for c in range(NCH - 1, NCH + 2):
                    step(c, g0, q0, a=False)

                G0 = value(pe, l * NG)

                def to_channels(j):
                    k0, w = GROUPS[j]
                    pe.wait_ge(agg_done, done(G0 + j))
                    pe.wait_ge(node_t_sb, done(G0 + (j - 2)))
                    pe.sem_inc(pe_passed, 1)
                    for k in range(w):
                        last = pe.transpose((pA, pH)[j % 2][0:H, k * NP:(k + 1) * NP], agg[j % 2][:, k, :], ident[0:NP, 0:NP])
                    last.then_inc(node_tp, 1)

                def linear1(j):
                    k0, w = GROUPS[j]
                    pe.wait_ge(node_t_sb, done(G0 + j))
                    pe.wait_ge(y_hat_done, done(G0 + (j - 2)))
                    for k in range(w):
                        last = pe.matmul(pX[j % 2][0:NP, k * H2:(k + 1) * H2], node_t[j % 2][:, k * NP:(k + 1) * NP],
                                         w1_now[:, :], start=True, stop=True)
                    last.then_inc(y_mm, 1)

                def hat_to_channels(j):
                    k0, w = GROUPS[j]
                    pe.wait_ge(y_hat_done, done(G0 + j))
                    if j < 2:
                        pe.wait_ge(back_sb, 2 * g0 + 2 * (NCH + PRE))
                    else:
                        pe.wait_ge(hid_done, done(G0 + (j - 2)))
                    for k in range(w):
                        last = pe.transpose(pT[j % 2][:, k * NP:(k + 1) * NP], y_hat[j % 2][:, k, :], ident[0:NP, 0:NP])
                    last.then_inc(hat_tp, 1)

                def linear2(j):
                    k0, w = GROUPS[j]
                    pe.wait_ge(hid_done, done(G0 + j))
                    pe.wait_ge(hres_done, done(G0 + (j - 2)))
                    for k in range(w):
                        at = pR[j % 2][0:NP, k * H:(k + 1) * H]
                        last = pe.matmul(at, hid_t[j % 2][:, k * NP:(k + 1) * NP], w2_now[:, :], start=True, stop=True)
                    last.then_inc(o_mm, 1)

                to_channels(0)
                linear1(0)
                to_channels(1)
                for j in range(NG):
                    hat_to_channels(j)
                    if j + 1 < NG:
                        linear1(j + 1)
                    if j + 2 < NG:
                        to_channels(j + 2)
                    linear2(j)

            layer(0, first_layer=True)
            with pe.Fori(1, L) as l:
                layer(l)

        @block.vector
        def _(dve):
            v = nc.vector
            v.memset(edge_w2[:, :], 0.0).then_inc(dve_consts, 1)
            v.memset(eps_col[:, :], LN_EPS).then_inc(dve_consts, 1)
            dve.wait_ge(consts, 8)
            v.tensor_copy(count_b[:, :], count_i[:, :])
            v.memset(zero_row[:, :], 0.0)
            v.memset(zeros_b[:, :], 0.0).then_inc(dve_consts, 1)
            for s in range(2):
                v.memset(node_t[s][H:H + 1, :], 1.0).then_inc(dve_consts, 1)
            dve.wait_ge(x_loaded, 16)
            for k in range(NK):
                v.bn_stats(stats_all[:, k, :], x_in[:, k, :])
            dve.drain()
            for k in range(NK):
                v.bn_aggr(mv_all[:, k, :], stats_all[:, k, :])
            dve.drain()
            v.tensor_copy(scr[:, :], mv_all[:, :, 1]).then_inc(enc_in, 1)
            dve.wait_ge(enc_in, 2)
            v.reciprocal(scr2[:, :], scr2[:, :])
            dve.drain()
            for k in range(NK):
                v.tensor_scalar(xn[:, k, :], x_in[:, k, :], mv_all[:, k, 0:1], scr2[:, k:k + 1], ALU.subtract, ALU.mult)
            dve.drain()
            v.tensor_scalar_max(xn[:, :, :], xn[:, :, :], 0.0).then_inc(enc_in, 1)

            v.memset(dst_win[0:1, :, 0:1], -1)
            dve.wait_ge(dst_in, 16 * 5)
            dve.drain()
            for h in range(2):
                v.tensor_tensor(drops[:, h, :], dst_win[:, h, 1:], dst_win[:, h, 0:CH], ALU.is_lt)
            dve.drain()
            v.tensor_reduce(drop_col[:, :], drops[:, :, :], AX.XY, ALU.max).then_inc(order_step, 1)

            for j, (k0, w) in enumerate(GROUPS):
                dve.wait_ge(enc_mm, j + 1)
                last = v.tensor_copy(z[:, k0:k0 + w, :], pX[j % 2][0:NP, 0:w * H].rearrange("p (k c) -> p k c", c=H))
                last.then_inc(enc_out, 1)
                if j == 0:
                    dve.wait_ge(order_tp, 1)
                    v.tensor_reduce(drop_flag[:, :], pT[0][0:1, 0:NCH], AX.X, ALU.max)
                    dve.drain()
                    v.tensor_copy(unsorted_i[:, :], drop_flag[:, :]).then_inc(order_known, 1)
            dve.wait_ge(enc_out, NG)
            dve.sem_inc(z_ready, 1)
            dve.sem_inc(hot_used, PRE)
            v.memset(hres[:, :, :], 0.0)
            for s in range(2):
                v.memset(M[s][:, :], 0.0)
                v.memset(S[s][:, :], 0.0)
                v.memset(W[s][:, :], 0.0)

            dve.wait_ge(order_known, 1)
            unsorted = dve.value_load(unsorted_i[0:1, 0:1], min_val=0, max_val=1)
            with dve.If(unsorted != 0):
                v.tensor_copy(node_f[:, :], node_i[:, :])
                v.memset(no_add[:, :], 0.0)
                v.memset(ones_col[:, :], 1.0)
                v.memset(next_rank[:, :], 0.0)
                dve.drain().then_inc(block_seen, 1)

                with dve.Fori(0, NSB) as b:
                    dve.wait_ge(block_in, b * 16 + 16)
                    v.tensor_copy(dst_all_f[:, :], dst_all[:, :])
                    dve.drain().then_inc(block_seen, 1)
                    for k in range(NK):
                        v.tensor_scalar(is_node[:, :], dst_all_f[:, :], node_f[:, k:k + 1], None, ALU.is_equal)
                        dve.drain()
                        v.tensor_reduce(block_count[:, k:k + 1], is_node[:, :], AX.X, ALU.add)
                        dve.drain()
                    v.tensor_tensor(next_rank[:, :], next_rank[:, :], block_count[:, :], ALU.add)
                    dve.drain()
                v.tensor_reduce(row_count[:, :], next_rank[:, :], AX.X, ALU.add)
                dve.drain().then_inc(rank_base, 1)
                v.tensor_tensor_scan(block_count[:, :], next_rank[:, :], no_add[:, 0:NK], -1.0, ALU.add, ALU.add)
                dve.drain()
                v.tensor_tensor(block_count[:, :], block_count[:, :], next_rank[:, :], ALU.subtract)
                dve.drain()
                dve.wait_ge(rank_base_mm, 1)
                v.tensor_scalar(next_rank[:, :], block_count[:, :], pH[0:NP, 0:1], None, ALU.add)
                dve.drain()
                with dve.Fori(0, NSB) as b:
                    dve.wait_ge(block_in, b * 16 + 16 * (NSB + 1))
                    v.tensor_copy(dst_all_f[:, :], dst_all[:, :])
                    v.memset(rank_part[:, :], 0.0)
                    dve.drain().then_inc(block_seen, 1)
                    for k in range(NK):
                        v.tensor_scalar(is_node[:, :], dst_all_f[:, :], node_f[:, k:k + 1], None, ALU.is_equal)
                        dve.drain()
                        v.tensor_tensor_scan(nth[:, :], is_node[:, :], no_add[:, :], next_rank[:, k:k + 1], ALU.add, ALU.add)
                        dve.drain()
                        v.tensor_copy(next_rank[:, k:k + 1], nth[:, SB - 1:SB])
                        v.tensor_tensor(is_node[:, :], is_node[:, :], nth[:, :], ALU.mult)
                        dve.drain()
                        v.tensor_tensor(rank_part[:, :], rank_part[:, :], is_node[:, :], ALU.add)
                        dve.drain()
                    dve.sem_inc(rank_summed, 1)
                    dve.wait_ge(rank_mm, b + 1)
                    dve.wait_ge(rank_stored, b * 16 + 16)
                    v.tensor_copy(rank_row[:, :], pT[0][0:1, 0:SB]).then_inc(rank_ready, 1)
                dve.wait_ge(cols_in, 48)
                with dve.Fori(0, ECOLS) as c:
                    dve.wait_ge(move_free, c + 1)
                    for to, table in ((move_rank, rank_cols), (move_src, src_cols), (move_dst, dst_cols)):
                        v.tensor_copy(to[:, :], table[:, bass.ds(c, 1)])
                    dve.drain().then_inc(move_ready, 1)
                dve.wait_ge(resorted_in, 16 * 5)
            with dve.Else():
                dve.wait_ge(cols_in, 16)

            for h in range(2):
                v.tensor_tensor(dst_d[:, h, :], dst_win[:, h, 1:], dst_win[:, h, 0:CH], ALU.not_equal)
            dve.drain()
            v.tensor_scalar(fall_sb[:, :, :], dst_d[:, :, :], FAR, None, ALU.mult).then_inc(fall_ready, 1)
            v.tensor_tensor(seam_fall[:, :], seam_dst[:, 0:1], seam_dst[:, 1:2], ALU.not_equal)
            dve.drain()
            v.tensor_scalar(seam_fall[:, :], seam_fall[:, :], FAR, None, ALU.mult)

            v.tensor_copy(dst_f[:, :], dst_cols[:, :])
            dve.drain()
            v.tensor_scalar(hi_f[:, :], dst_f[:, :], 1.0 / NK, -(NK // 2) / NK, ALU.mult, ALU.add)
            dve.drain()
            v.tensor_scalar(hi_f[:, :], hi_f[:, :], ROUND, None, ALU.add)
            dve.drain()
            v.tensor_scalar(hi_f[:, :], hi_f[:, :], -ROUND, None, ALU.add)
            dve.drain()
            v.tensor_copy(hi_b[:, :], hi_f[:, :])
            v.scalar_tensor_tensor(out=lo_b[:, :], in0=hi_f[:, :], scalar=-float(NK), in1=dst_f[:, :], op0=ALU.mult, op1=ALU.add)
            dve.drain()
            dve.wait_ge(par_in, 16 * N_PAR)
            for counter in (m_done, d_done, du_done, rex_done, sw_done, agg_done, y_hat_done, hres_done):
                dve.sem_inc(counter, PRE)
            for mean, weight, n in ((w1_mean, w1b, H2), (w2_mean, w2_all, H), (b2_mean, b2_all, H)):
                v.tensor_reduce(mean[:, :], weight[:, :, :], AX.X, ALU.add)
                dve.drain()
                v.tensor_scalar(mean[:, :], mean[:, :], 1.0 / n, None, ALU.mult)
                dve.drain()
                v.tensor_tensor(weight[:, :, :], weight[:, :, :], mean[:, :, None].to_broadcast(list(weight.shape)), ALU.subtract)
            dve.drain()

            def layer(l, first_layer=False):
                one = bass.ds(l, 1)
                v.tensor_copy(t_now[:, :], t_all[:, one])
                v.tensor_copy(w1_now[:, :], w1b[:, one, :].rearrange("p o n -> p (o n)"))
                v.tensor_copy(w2_now[:, :], w2_all[:, one, :].rearrange("p o n -> p (o n)"))
                v.tensor_copy(g1_now[:, :], g1_all[:, one])
                v.tensor_copy(bb1_now[:, :], bb1_all[:, one])
                v.tensor_copy(lng_now[:, :], lng_all[:, one, :].rearrange("p o n -> p (o n)"))
                v.tensor_copy(lnb_now[:, :], lnb_all[:, one, :].rearrange("p o n -> p (o n)"))
                dve.drain().then_inc(layer_par, 1)
                v.tensor_tensor(hres[:, :, :], hres[:, :, :], b2_all[:, one, :].to_broadcast([NP, NK, H]), ALU.add)

                def step(c, g, q, b=True, d=True):
                    s, s1 = c % 2, (c - 1) % 2
                    g_b, g_d = g + c, g + (c - 1)
                    if b:
                        dve.wait_ge(u_done, done(g_b))
                        dve.wait_ge(m_stored[s], (q + c // 2) * 16 + 16)
                        v.tensor_tensor_scan(M[s][:, 1:CH + 1], pR[s][:, :], du[s][:, 1, :], M[s1][:, CH:CH + 1], ALU.add, ALU.max)
                        v.tensor_copy(M[s][:, 0:1], M[s1][:, CH:CH + 1]).then_inc(m_done, 1)
                    if d:
                        dve.wait_ge(ex_done, done(g_d))
                        dve.wait_ge(sw_done, done(g_d - 1))
                        v.tensor_tensor(rex[:, :], r[s1][:, :], ex[s1][:, 1, :], ALU.mult).then_inc(rex_done, 1)
                    if b:
                        dve.wait_ge(m_done, done(g_b))
                        v.tensor_tensor(du[s][:, 0, :], pR[s][:, :], M[s][:, 0:CH], ALU.add).then_inc(d_done, 1)
                    if d:
                        dve.wait_ge(back_tp, 2 * g_d + (2 * PRE - 2))
                        v.tensor_tensor_scan(S[s1][:, :], ex[s1][:, 0, :], ex[s1][:, 1, :], S[s][:, CH - 1:CH], ALU.mult, ALU.add)
                    if b:
                        dve.wait_ge(d_done, done(g_b))
                        v.tensor_tensor(du[s][:, :, :], du[s][:, :, :], M[s][:, None, 1:CH + 1].to_broadcast([P, 2, CH]),
                                        ALU.subtract).then_inc(du_done, 1)
                    if d:
                        dve.wait_ge(rex_done, done(g_d))
                        v.tensor_tensor_scan(W[s1][:, :], ex[s1][:, 0, :], rex[:, :], W[s][:, CH - 1:CH], ALU.mult, ALU.add).then_inc(sw_done, 1)

                g0, q0 = value(dve, l * NCH), value(dve, l * (NCH // 2))
                step(0, g0, q0, d=False)
                step(1, g0, q0)
                i0 = 1
                if first_layer:
                    i0 += NHB // 2
                    with dve.Fori(1, i0) as i:
                        g, q = dve.snap(g0 + i * 2), dve.snap(q0 + i)
                        for c in range(2):
                            step(c, g, q)
                            dve.wait_ge(hot_used, done(i * 2 + (c - 4)))
                            cols = bass.ds(i * (2 * HB) + (c - 2) * HB, HB)
                            v.tensor_tensor(hot_hi[c][:, :, :], count_b[:, None, 0:NP].to_broadcast([NP, HB, NP]),
                                            hi_b[:, cols][:, :, None].to_broadcast([NP, HB, NP]), ALU.is_equal)
                            v.tensor_tensor(hot_lo[c][:, :, :], count_b[:, None, 0:NK].to_broadcast([NP, HB, NK]),
                                            lo_b[:, cols][:, :, None].to_broadcast([NP, HB, NK]), ALU.is_equal).then_inc(hot_ready, 1)
                    dve.wait_ge(hist_done, 1)
                    v.tensor_copy(hist[:, :], pH[0:NP, 0:NK])
                    dve.drain()
                    v.tensor_reduce(hist_sum[:, :], hist[:, :], AX.X, ALU.add).then_inc(cum_step, 1)
                    v.memset(scr[:, :], 0.0)
                    dve.drain()
                    v.tensor_tensor_scan(cum[:, :], hist[:, :], scr[:, :], 0.0, ALU.add, ALU.add)
                    v.tensor_scalar(has_edges[:, :], hist[:, :], 0.0, None, ALU.is_gt)
                    dve.wait_ge(cum_mm, 1)
                    dve.drain()
                    v.tensor_scalar(cum[:, :], cum[:, :], pH[0:NP, 64:65], None, ALU.add)
                    dve.drain()
                    v.tensor_scalar(scr[:, :], cum[:, :], float(HALF_AT), 1e9, ALU.is_le, ALU.mult)
                    dve.drain()
                    v.tensor_tensor(scr[:, :], scr[:, :], cum[:, :], ALU.add)
                    dve.drain()
                    v.tensor_reduce(seam_col[:, :], scr[:, :], AX.X, ALU.min).then_inc(cum_step, 1)
                    v.tensor_scalar(scr2[:, :], cum[:, :], -1.0, 0.0, ALU.add, ALU.max)
                    dve.drain()
                    v.tensor_scalar(scr[:, :], scr2[:, :], float(HALF_AT), float(SW_SHIFT), ALU.is_ge, ALU.mult)
                    dve.drain()
                    v.tensor_tensor(scr[:, :], scr[:, :], scr2[:, :], ALU.add)
                    dve.drain()
                    v.tensor_scalar(scr[:, :], scr[:, :], -float(EMPTY_ROW), None, ALU.add)
                    dve.drain()
                    v.tensor_tensor(scr[:, :], scr[:, :], has_edges[:, :], ALU.mult)
                    dve.drain()
                    v.tensor_scalar(scr[:, :], scr[:, :], float(EMPTY_ROW), None, ALU.add)
                    dve.drain()
                    v.tensor_copy(row_idx[:, :], scr[:, :])
                    dve.wait_ge(cum_mm, 2)
                    v.tensor_reduce(seam_row[:, 0:1], pH[0:1, 128:128 + NP], AX.X, ALU.min)
                    dve.drain()
                    v.tensor_scalar(seam_row[:, 1:2], seam_row[:, 0:1], -float(1 + HALF_AT), None, ALU.add)
                    dve.drain()
                    v.tensor_copy(seam_end[:, :], seam_row[:, 1:2]).then_inc(seam_known, 1)
                with dve.Fori(i0, NCH // 2 - 1) as i:
                    g, q = dve.snap(g0 + i * 2), dve.snap(q0 + i)
                    for c in range(2):
                        step(c, g, q)
                step(NCH - 2, g0, q0)
                step(NCH - 1, g0, q0)
                step(NCH, g0, q0, b=False)

                last_s = (NCH - 1) % 2
                dve.wait_ge(sw_done, g0 + (NCH + PRE))
                dve.wait_ge(seam_in, l * 32 + 32)
                v.tensor_tensor(seam_m[:, 0:1], M[last_s][0:H, CUT_COL + 1:CUT_COL + 2], seam_fall[:, :], ALU.add)
                dve.drain()
                v.tensor_tensor(seam_x[:, :], seam_m[:, 0:1], seam_m[:, 1:2], ALU.max)
                dve.drain()
                v.tensor_scalar(seam_m[:, :], seam_m[:, :], seam_x[:, :], None, ALU.subtract).then_inc(seam_max, 1)
                dve.wait_ge(seam_exp, l + 1)
                v.tensor_scalar(seam_sw1[:, :], seam_sw1[:, :], seam_e[:, 1:2], None, ALU.mult)
                dve.drain()
                for n, scanned in enumerate((S, W)):
                    v.scalar_tensor_tensor(out=seam_sw[:, n:n + 1], in0=scanned[last_s][0:H, CUT_COL:CUT_COL + 1],
                                           scalar=seam_e[:, 0:1], in1=seam_sw1[:, n:n + 1], op0=ALU.mult, op1=ALU.add)
                dve.drain().then_inc(seam_done, 1)

                G0 = value(dve, l * NG)

                def aggregate(j):
                    k0, w = GROUPS[j]
                    ks = slice(k0, k0 + w)
                    dve.wait_ge(node_in[j], l * (16 * w) + 16 * w)
                    dve.wait_ge(node_tp, done(G0 + (j - 2)))
                    a = agg[j % 2][:, 0:w, :]
                    v.tensor_scalar(rden[:, 0:w, :], node_sw[:, ks, 0, :], DEN_EPS, None, ALU.add)
                    v.scalar_tensor_tensor(out=a, in0=node_sw[:, ks, 0, :], scalar=MSG_EPS, in1=node_sw[:, ks, 1, :], op0=ALU.mult, op1=ALU.add)
                    dve.drain()
                    v.reciprocal(rden[:, 0:w, :], rden[:, 0:w, :])
                    dve.drain()
                    v.tensor_tensor(a, a, rden[:, 0:w, :], ALU.mult)
                    dve.drain()
                    v.tensor_tensor(a, a, z[:, ks, :], ALU.add).then_inc(agg_done, 1)

                def norm1(j):
                    w = GROUPS[j][1]
                    dve.wait_ge(sd1_done, done(G0 + j))
                    dve.wait_ge(hat_tp, done(G0 + (j - 2)))
                    v.reciprocal(rs1[j % 2][:, 0:w], sd1[j % 2][:, 0:w])
                    dve.drain()
                    v.tensor_tensor(y_hat[j % 2][:, 0:w, :], pX[j % 2][0:NP, 0:w * H2].rearrange("p (k c) -> p k c", c=H2),
                                    rs1[j % 2][:, 0:w, None].to_broadcast([NP, w, H2]), ALU.mult).then_inc(y_hat_done, 1)

                def residual(j):
                    k0, w = GROUPS[j]
                    ks = slice(k0, k0 + w)
                    dve.wait_ge(o_mm, done(G0 + j))
                    v.tensor_tensor(hres[:, ks, :], pR[j % 2][0:NP, 0:w * H].rearrange("p (k c) -> p k c", c=H), hres[:, ks, :],
                                    ALU.add).then_inc(hres_done, 1)

                def norm2(j):
                    k0, w = GROUPS[j]
                    ks = slice(k0, k0 + w)
                    dve.wait_ge(sd2_done, done(G0 + j))
                    v.reciprocal(rs2[j % 2][:, 0:w], sd2[j % 2][:, 0:w])
                    dve.drain()
                    for k in range(w):
                        v.scalar_tensor_tensor(out=z[:, k0 + k, :], in0=hres[:, k0 + k, :], scalar=rs2[j % 2][:, k:k + 1],
                                               in1=lng_now[:, :], op0=ALU.mult, op1=ALU.mult)
                    dve.drain()
                    v.tensor_tensor(z[:, ks, :], z[:, ks, :], lnb_now[:, None, :].to_broadcast([NP, w, H]), ALU.add)
                    dve.drain()
                    v.tensor_scalar_max(z[:, ks, :], z[:, ks, :], 0.0)

                aggregate(0)
                aggregate(1)
                norm1(0)
                aggregate(2)
                for j in range(NG + 1):
                    if j >= 1:
                        residual(j - 1)
                    if j + 1 < NG:
                        norm1(j + 1)
                    if j >= 2:
                        norm2(j - 2)
                    if j + 3 < NG:
                        aggregate(j + 3)
                norm2(NG - 1)
                dve.drain().then_inc(z_ready, 1)

            layer(0, first_layer=True)
            with dve.Fori(1, L) as l:
                layer(l)

            v.tensor_tensor(x_in[:, :, :], x_in[:, :, :], z[:, :, :], ALU.add).then_inc(out_ready, 1)


_INS = ['x', 'src', 'dst', 'edge_attr_64', 'L0_gnn_enc_node_w', 'L0_gnn_enc_node_b', 'L0_gnn_enc_edge_w', 'L0_gnn_enc_edge_b',
        'L0_gnn_ln_g', 'L0_gnn_ln_b', 'L0_gnn_mlp1_w', 'L0_gnn_mlp1_b', 'L0_gnn_mlp_ln_g', 'L0_gnn_mlp_ln_b',
        'L0_gnn_mlp2_w', 'L0_gnn_mlp2_b', 'L0_gnn_t']


def kernel(**inputs):
    import numpy as _np
    import concourse.bacc as _bacc
    from concourse import mybir as _mybir
    from concourse.bass_utils import run_bass_kernel_spmd as _run

    nc = _bacc.Bacc("TRN2", target_bir_lowering=False, num_devices=1)
    arrays, args = {}, []
    for name in _INS:
        a = _np.ascontiguousarray(inputs[name])
        arrays[f"in_{name}_dram"] = a
        args.append(nc.dram_tensor(f"in_{name}_dram", a.shape, _mybir.dt.from_np(a.dtype), kind="ExternalInput").ap())
    args.append(nc.dram_tensor("out_0_dram", (N, H), _mybir.dt.float32, kind="ExternalOutput").ap())
    program(nc, *args)
    r = _run(nc, [arrays], core_ids=[0])
    return r.results[0]["out_0_dram"]
```
